# Optimizing a Trainium2 kernel written in Bass

```python
import numpy as np
import jax
import jax.numpy as jnp

def _softmax(x, axis=-1):
    return jax.nn.softmax(x, axis=axis)

def _gelu(x):
    return jax.nn.gelu(x, approximate=True)

def _silu(x):
    return jax.nn.silu(x)

def _sigmoid(x):
    return jax.nn.sigmoid(x)

def _layernorm(x, axis=-1, eps=1e-05):
    m = jnp.mean(x, axis=axis, keepdims=True)
    v = jnp.var(x, axis=axis, keepdims=True)
    return (x - m) / jnp.sqrt(v + eps)

def _scatter_add(tgt, idx, src, axis=0):
    return tgt.at[idx].add(src)

def _segment_sum(src, seg, n):
    return jax.ops.segment_sum(src, seg, n)
kernel_name = 'mk_gnn_resnorm_d2_gnn_r64_e41d4e'

def setup_inputs(seed: int=0):
    np.random.seed(seed)
    _w = jnp.asarray

    def _rec_inputs():
        import jax
        import jax.numpy as jnp
        _gk = jax.random.key(seed)
        x = -0.0005121 + 1.001 * jax.random.normal(jax.random.fold_in(_gk, 1), (100000, 32), jnp.float32)
        src = jax.random.randint(jax.random.fold_in(_gk, 2), (50000,), 0, 100000, jnp.int32)
        dst = jnp.minimum((100000 * jax.random.uniform(jax.random.fold_in(_gk, 3), (50000,)) ** 2.0).astype(jnp.int32), 99999)
        _o = jnp.argsort(dst, stable=True)
        src = src[_o]
        dst = dst[_o]
        edge_attr_32 = jax.random.uniform(jax.random.fold_in(_gk, 12), (50000, 32), jnp.float32, 0.0, 1)
        edge_weight = jax.random.uniform(jax.random.fold_in(_gk, 14), (50000,), jnp.float32, 0.0, 0.999999)
        node_vec = jax.random.uniform(jax.random.fold_in(_gk, 15), (100000,), jnp.float32, 0.0, 1)
        node_vec_n2 = jax.random.uniform(jax.random.fold_in(_gk, 16), (100000,), jnp.float32, 0.0, 1)
        node_vec_n3 = jax.random.uniform(jax.random.fold_in(_gk, 17), (100000,), jnp.float32, 0.0, 1)
        return (x, src, dst, edge_attr_32, edge_weight, node_vec, node_vec_n2, node_vec_n3)
    x, src, dst, edge_attr_32, edge_weight, node_vec, node_vec_n2, node_vec_n3 = _rec_inputs()

    def _L0_gnn_setup():
        import jax, jax.numpy as jnp
        import numpy as np
        N = 100000
        E = 25000
        DIMS = [32, 32, 32]
        K = 3
        NEG_SLOPE = 0.01
        EPS = 1e-05

        def _gcn_norm(src, dst, w, n):
            deg = jax.ops.segment_sum(w, dst, num_segments=n)
            dinv = jnp.where(deg > 0, jax.lax.rsqrt(deg), 0.0)
            return dinv[src] * w * dinv[dst]

        def _tagconv(x, src, dst, norm, W, b, n):
            out = x @ W[0]
            h = x
            for k in range(1, W.shape[0]):
                h = jax.ops.segment_sum(norm[:, None] * h[src], dst, num_segments=n)
                out = out + h @ W[k]
            return out + b

        def _batchnorm_nodes(x, gamma, beta):
            mu = jnp.mean(x, axis=1, keepdims=True)
            var = jnp.mean((x - mu) ** 2, axis=1, keepdims=True)
            return (x - mu) * jax.lax.rsqrt(var + EPS) * gamma[:, None] + beta[:, None]
        key = jax.random.key(seed)
        ks = jax.random.split(key, 8)
        x = jax.random.normal(ks[0], (N, DIMS[0]), jnp.float32)
        edge_index = jax.random.randint(ks[1], (2, E), 0, N, jnp.int64)
        edge_weights = jax.random.uniform(ks[2], (E,), jnp.float32)
        feature_mask = jax.random.uniform(ks[3], (N,), jnp.float32)
        W0 = jax.random.normal(ks[4], (K + 1, DIMS[0], DIMS[1]), jnp.float32) / np.float32(np.sqrt(DIMS[0]))
        b0 = jnp.zeros((DIMS[1],), jnp.float32)
        W1 = jax.random.normal(ks[5], (K + 1, DIMS[1], DIMS[2]), jnp.float32) / np.float32(np.sqrt(DIMS[1]))
        b1 = jnp.zeros((DIMS[2],), jnp.float32)
        gamma0 = jnp.ones((N,), jnp.float32)
        beta0 = jnp.zeros((N,), jnp.float32)
        return dict(x=x, edge_index=edge_index, edge_weights=edge_weights, feature_mask=feature_mask, W0=W0, b0=b0, W1=W1, b1=b1, gamma0=gamma0, beta0=beta0)
    _L0_gnn_all = _L0_gnn_setup()
    _L0_gnn_in = {k: v for k, v in _L0_gnn_all.items() if k in ('W0', 'b0', 'W1', 'b1')}
    del _L0_gnn_all

    def _L1_gnn_setup():
        import jax, jax.numpy as jnp
        import numpy as np
        N_NODES = 100000
        N_EDGES = 25000
        D_FEAT = 32
        key = jax.random.key(seed)
        k1, k2, k3, k4 = jax.random.split(key, 4)
        rel = jax.random.normal(k1, (N_NODES, D_FEAT), dtype=jnp.float32)
        pattern = jax.random.uniform(k2, (N_EDGES, D_FEAT), dtype=jnp.float32)
        src = jax.random.randint(k3, (N_EDGES,), 0, N_NODES, dtype=jnp.int64)
        dst = jax.random.randint(k4, (N_EDGES,), 0, N_NODES, dtype=jnp.int64)
        return {'rel': rel, 'pattern': pattern, 'src': src, 'dst': dst}
    _L1_gnn_all = _L1_gnn_setup()
    _L1_gnn_in = {k: v for k, v in _L1_gnn_all.items() if k in ()}
    del _L1_gnn_all
    return {'x': x, 'src': src, 'dst': dst, 'edge_attr_32': edge_attr_32, 'edge_weight': edge_weight, 'node_vec': node_vec, 'node_vec_n2': node_vec_n2, 'node_vec_n3': node_vec_n3, 'L0_gnn_W0': _L0_gnn_in['W0'], 'L0_gnn_b0': _L0_gnn_in['b0'], 'L0_gnn_W1': _L0_gnn_in['W1'], 'L0_gnn_b1': _L0_gnn_in['b1']}

def reference(x, src, dst, edge_attr_32, edge_weight, node_vec, node_vec_n2, node_vec_n3, L0_gnn_W0, L0_gnn_b0, L0_gnn_W1, L0_gnn_b1):
    import jax
    import jax.numpy as jnp

    def _L0_gnn_ref(x, edge_index, edge_weights, feature_mask, W0, b0, W1, b1, gamma0, beta0):
        import jax, jax.numpy as jnp
        import numpy as np
        N = 100000
        E = 25000
        DIMS = [32, 32, 32]
        K = 3
        NEG_SLOPE = 0.01
        EPS = 1e-05

        def _gcn_norm(src, dst, w, n):
            deg = jax.ops.segment_sum(w, dst, num_segments=n)
            dinv = jnp.where(deg > 0, jax.lax.rsqrt(deg), 0.0)
            return dinv[src] * w * dinv[dst]

        def _tagconv(x, src, dst, norm, W, b, n):
            out = x @ W[0]
            h = x
            for k in range(1, W.shape[0]):
                h = jax.ops.segment_sum(norm[:, None] * h[src], dst, num_segments=n)
                out = out + h @ W[k]
            return out + b

        def _batchnorm_nodes(x, gamma, beta):
            mu = jnp.mean(x, axis=1, keepdims=True)
            var = jnp.mean((x - mu) ** 2, axis=1, keepdims=True)
            return (x - mu) * jax.lax.rsqrt(var + EPS) * gamma[:, None] + beta[:, None]
        src, dst = (edge_index[0], edge_index[1])
        norm = _gcn_norm(src, dst, edge_weights, N)
        out = _tagconv(x, src, dst, norm, W0, b0, N)
        out = _batchnorm_nodes(out, gamma0, beta0)
        out = jnp.where(out > 0, out, NEG_SLOPE * out)
        out = _tagconv(out, src, dst, norm, W1, b1, N)
        return out * feature_mask[:, None]

    def _L1_gnn_ref(rel, pattern, src, dst):
        import jax, jax.numpy as jnp
        import numpy as np
        N_NODES = 100000
        N_EDGES = 25000
        D_FEAT = 32
        msg = rel[src] * pattern
        sums = jax.ops.segment_sum(msg, dst, num_segments=N_NODES)
        deg = jax.ops.segment_sum(jnp.ones((msg.shape[0],), msg.dtype), dst, num_segments=N_NODES)
        h_N = sums / jnp.maximum(deg, 1.0)[:, None]
        return h_N + rel
    edge_index = jnp.stack([src, dst])
    x = _layernorm(x + _L0_gnn_ref(x, edge_index, edge_weight, node_vec, L0_gnn_W0, L0_gnn_b0, L0_gnn_W1, L0_gnn_b1, node_vec_n2, node_vec_n3), axis=-1)
    x = _layernorm(x + _L1_gnn_ref(x, edge_attr_32, src, dst), axis=-1)
    return x

_drawn_inputs = setup_inputs


def setup_inputs(seed=0):
    import zlib

    import numpy as np

    out = dict(_drawn_inputs(seed))
    spreads = {'L0_gnn_b0': (0.0, 0.29), 'L0_gnn_b1': (0.0, 0.1)}
    factors = {}
    for name, (base, spread) in spreads.items():
        noise = np.random.default_rng([zlib.crc32(name.encode()), seed]).standard_normal(out[name].shape)
        drawn = base * np.exp(spread * noise) if base else spread * noise
        out[name] = jnp.asarray(drawn.astype(out[name].dtype))
    for name, factor in factors.items():
        out[name] = (out[name] * factor).astype(out[name].dtype)
    return out
```

```python
import concourse.bass as bass
from concourse import mybir
from contextlib import ExitStack

F32 = mybir.dt.float32
I32 = mybir.dt.int32
ALU = mybir.AluOpType
ACT = mybir.ActivationFunctionType
AX = mybir.AxisListType

P = 128
N = 100000
E = 50000
D = 32
HOPS = 3
EPS = 1e-5
SLOPE = 0.01

J = 392
EP = P * J
EB = 28
JC = 400
CB = 8
CN = JC // (2 * CB)
JX = JC + 2 * CB
NB = 56
NBLK = 14
NP = P * NB * NBLK
LASTP, LASTC = (N - (NBLK - 1) * P * NB) // NB, (N - (NBLK - 1) * P * NB) % NB
ITS = 7
PADV = 200000.0
TROWS = P * JC
LT = 4
ST = 2
PER = 16 * CB // ST
LEAD = 6
HT = 20
GC = 4


def gnn_program(nc, x, src, dst, attr, weight, nv, gamma, beta, W0, b0, W1, b1, out):
    ctx = ExitStack()
    with ctx:
        def sb(name, shape, dt=F32):
            return ctx.enter_context(nc.sbuf_tensor(name, shape, dt))

        def sem(name):
            return ctx.enter_context(nc.semaphore(name))

        def sems(name):
            return [sem(f"{name}{s}") for s in range(2)]

        def dram(name, shape, dt=F32):
            return nc.dram_tensor(name, shape, dt, kind="Internal").ap()

        e_src = dram("e_src", (EP,), I32)
        e_dst = dram("e_dst", (EP,), I32)
        e_w = dram("e_w", (EP,))
        e_attr = dram("e_attr", (EP, D))
        node_lasts = [dram(f"node_lasts{k}", (NP + P, 1)) for k in range(LT)]
        node_last = dram("node_last", (NP + P, 1))
        edge_info = dram("edge_info", (1 + EP, 2))
        node_sum = [dram(f"node_sum{k}", (NP + P, D)) for k in range(ST)]
        agg_sum = [dram(f"agg_sum{k}", (NP + P, D)) for k in range(ST)]
        node_tab = dram("node_tab", (NP, D))
        hop_tab = [dram(f"hop_tab{k}", (1 + TROWS + P, D)) for k in range(HOPS - 1)]

        ident = sb("ident", [P, P])
        before = sb("before", [P, P])
        after = sb("after", [P, P])
        ones = sb("ones", [P, J])
        zeros = sb("zeros", [P, (NP + P) // P])
        col_i = sb("col_i", [P, JC])
        part_c = sb("part_c", [P, 4])
        padi = sb("padi", [1, P * J - E], I32)
        bd = sb("bd", [P, 2 * (HOPS + 1) * P])
        brow = sb("brow", [1, 2 * 512])

        e_i = sb("e_i", [P, 2, J], I32)
        same = sb("same", [P, J])
        rcnt = sb("rcnt", [P, J])
        sidx = sb("sidx", [P, J], I32)
        mat = sb("mat", [P, P])
        mat2 = sb("mat2", [P, P])
        sm = sb("sm", [P, 48])
        ci32 = sb("ci32", [P, 4], I32)
        w1 = sb("w1", [P, JX])
        w2 = sb("w2", [P, JX])
        gidx = sb("gidx", [P, JX], I32)
        srcc = sb("srcc", [P, JX], I32)
        ridx = sb("ridx", [P, JX], I32)
        uidx = sb("uidx", [P, JX], I32)
        sdd = sb("sdd", [P, JC])
        lastc = sb("lastc", [P, JC])
        samec = sb("samec", [P, JC])
        maskc = sb("maskc", [P, JX // CB * (CB + 1)])
        maske = sb("maske", [P, (J // EB + 2) * (EB + 1)])
        sdh = sb("sdh", [P, 1])
        matc = sb("matc", [P, P])
        n_it = sb("n_it", [1, 2], I32)

        nd = sb("nd", [P, NBLK * NB * D])
        nvs = sb("nvs", [P, NBLK * NB])
        carry = sb("carry", [P, D])
        istage = [sb(f"istage{s}", [P, EB], I32) for s in range(2)]
        eidx_ = [sb(f"eidx{s}", [P, EB], I32) for s in range(2)]
        work = sb("work", [P, 2 * 4 * NB * D])
        W = NB * D

        def slotv(s, off, n):
            return work[:, s * 4 * W + off:s * 4 * W + off + n]

        g_ = [slotv(s, 0, EB * D) for s in range(2)]
        v_ = [slotv(s, 896, (EB + 1) * D) for s in range(2)]
        s_ = [slotv(s, 1824, (EB + 1) * D) for s in range(2)]
        m_ = [slotv(s, 2752, (EB + 1) * D) for s in range(2)]
        r_ = [slotv(s, 3680, EB * D) for s in range(2)]
        a_ = [slotv(s, 4576, EB * D) for s in range(2)]
        tl_ = [slotv(s, 4576, (HOPS - 1) * CB * D) for s in range(2)]
        hb_ = [slotv(s, 5088, CB * D) for s in range(2)]
        tt_ = [slotv(s, 5344, HOPS * P) for s in range(2)]
        ub = [slotv(s, 0, W) for s in range(2)]
        cb = [slotv(s, W, W) for s in range(2)]
        sq = [slotv(s, 2 * W, W) for s in range(2)]
        xb = [slotv(s, 3 * W, W) for s in range(2)]
        at = [0, 4 * W]

        def early(s, *shape, dt=F32):
            n = 1
            for d in shape:
                n *= d
            t = work[:, at[s]:at[s] + n]
            at[s] += n
            assert at[s] <= s * 4 * W + 3 * W
            if dt != F32:
                t = t.bitcast(dt)
            if len(shape) == 2:
                t = t.rearrange("p (a b) -> p a b", a=shape[0])
            return t

        pay = early(0, 5, JC)
        sh = early(0, 2, JC, dt=I32)
        mv = early(0, JC, dt=I32)
        t_e = early(0, JC)
        t_f = early(0, JC)
        lb = early(0, 4 * P)
        live = early(0, JC)
        d_e = early(1, J)
        w_e = early(1, J)
        edge_no = early(1, J)
        last = early(1, J)
        head = early(1, J)
        deg = early(1, J)
        cnt = early(1, J)
        ddst = early(1, J)
        rv = early(1, J)
        eg = early(1, JX, 2)
        ei = early(1, J, 2)

        lasts = [work[:, t * (NP + P) // P:(t + 1) * (NP + P) // P] for t in range(LT)]

        xt = [sb(f"xt{i}", [P, 4 * P]) for i in range(2)]
        gb = [sb(f"gb{s}", [P, 2 * NB]) for s in range(2)]
        st = [sb(f"st{s}", [P, 2 * NB]) for s in range(2)]

        ps_t = [ctx.enter_context(nc.psum_tensor(f"ps_t{i}", [P, 512], F32)) for i in range(2)]
        ps_o = [ctx.enter_context(nc.psum_tensor(f"ps_o{i}", [P, 512], F32)) for i in range(2)]
        ps_b = ctx.enter_context(nc.psum_tensor("ps_b", [P, 512], F32))
        ps_c = ctx.enter_context(nc.psum_tensor("ps_c", [P, 512], F32))

        def b_split(t, r):
            return t.rearrange("(a b) -> a b", a=r)

        def ev(t):
            return t.rearrange("(p j) -> p j", p=P)

        attr_v = e_attr.rearrange("(p j) f -> p (j f)", p=P)

        def hop_rows(k):
            return hop_tab[k][1:1 + TROWS, :].rearrange("(p j) f -> p (j f)", p=P)

        def node_rows(t, b):
            return t[bass.ds(b * (P * NB), P * NB), :].rearrange("(p c) f -> p (c f)", p=P)

        def fj(t, n):
            return t[:, 0:D * n].rearrange("p (f j) -> p f j", f=D)

        def jf(t, n):
            return t[:, 0:D * n].rearrange("p (j f) -> p f j", f=D)

        def over_f(t):
            return t.unsqueeze(1).to_broadcast([P, D, t.shape[1]])

        def over_row(t):
            return t.unsqueeze(2).to_broadcast([P, t.shape[1], D])

        def rows(t, n=NB):
            return t.rearrange("p (c f) -> p c f", f=D)

        phase_done = sem("phase_done")
        phase_no = {}

        def phase_end(eng, name):
            phase_no[name] = phase_no.get(name, 0) + 1
            eng.drain().then_inc(phase_done, 1)
            eng.wait_ge(phase_done, 5 * phase_no[name])

        def so_far(round, turns, it, per, more, extra=0):
            at = it * per + more + round * extra
            return at if round == 0 else turns * (round * per) + at

        class Chain:

            def __init__(self, eng, name):
                self.eng, self.sem, self.n, self.per, self.it = eng, sem(name), 0, 0, 0
                self.round, self.turns = 0, 0

            def begin(self, it, round=0, turns=0):
                self.it, self.n, self.round, self.turns = it, 0, round, turns

            def link(self, ins):
                self.n += 1
                ins.then_inc(self.sem, 1)
                self.eng.wait_ge(self.sem, so_far(self.round, self.turns, self.it, self.per, self.n))

            def end(self):
                self.per = self.n

        def rolled(eng, count, body, upto=None, last_apart=0):
            body(0)
            with eng.Fori(1, count - last_apart) as it:
                if upto is None:
                    body(it)
                else:
                    with eng.If(it < upto):
                        body(it)
            for it in range(count - last_apart, count):
                body(it)

        def first(it):
            return isinstance(it, int) and it == 0

        copied = sem("copied")
        zeroed = sem("zeroed")
        tabs0 = sem("tabs0")
        big0 = sem("big0")
        consts = sem("consts")
        loaded = sem("loaded")
        cols_ready = sem("cols_ready")
        spread = sem("spread")
        info_out = sem("info_out")
        wts = sem("wts")
        consts_ready = sem("consts_ready")
        bd0 = sem("bd0")
        act_own = sem("act_own")
        root_in = sem("root_in")
        root_out = sem("root_out")
        lasts_in = sem("lasts_in")
        lasts_sum = sem("lasts_sum")
        gb_in = sems("gb_in")
        l0 = sem("l0")

        def hop_sems(tag):
            return dict(gathered=sems(f"gat_{tag}"), staged=sems(f"stg_{tag}"), masked=sems(f"msk_{tag}"),
                        scanned=sem(f"scn_{tag}"), rowed=sem(f"row_{tag}"), written=sems(f"wrt_{tag}"),
                        carried=sem(f"car_{tag}"))

        hs = hop_sems("hop")
        hop_chain = []
        fs = dict(gathered=sems("fga"), staged=sems("fst"), masked=sems("fmk"), scanned=sem("fsc"), rowed=sem("frw"),
                  carried=sem("fca"), loaded=sems("fld"), transposed=sem("ftr"), copied=sem("fcp"), mult=sem("fmm"),
                  ready=sems("frd"), scattered=[sem(f"fsx{t}") for t in range(ST)])
        fold_chain = []
        rs = dict(staged=sems("rstg"), scattered=[sem(f"rsct{t}") for t in range(LT)])
        rg = dict(staged=sems("gstg"), gathered=sems("ggat"))
        eg_s = dict(staged=sems("estg"), gathered=sems("egat"))
        a0 = dict(xl=sems("a0x"), tr=sem("a0t"), cp=sem("a0c"), mm=sem("a0m"), ev=sem("a0e"))
        dense = [dict(ul=sems(f"dul{i}_"), add=sem(f"dad{i}"), cen=sem(f"dce{i}"), sq=sem(f"dsq{i}"), var=sem(f"dva{i}"), both=sem(f"dbo{i}"),
                      root=sem(f"dro{i}"),
                      done=sem(f"ddn{i}"), stored=sems(f"dst{i}_"), chain=f"dch{i}") for i in range(3)]
        bs = dict(xl=sems("bxl"), zs=sems("bzs"), tr=sem("btr"), cp=sem("bcp"), mm=sem("bmm"), ev=sem("bev"))
        ls = dict(attr=sems("lat"), gathered=sems("lga"), staged=sems("lst"), masked=sems("lmk"), scanned=sem("lsc"),
                  ready=sems("lrd"), scattered=sems("lsx"), carried=sem("lca"))

        block = ctx.enter_context(nc.Block())

        def hop_sp(sp, h, n):
            q, k = hs, h % (HOPS - 1)

            def body(it):
                for s in range(2):
                    sp.wait_ge(q["rowed"], so_far(h, n, it, 2, s + 1))
                    sp.dma_start(hop_rows(k)[:, bass.ds(it * (2 * CB * D) + s * CB * D, CB * D)],
                                 r_[s][:, 0:CB * D]).then_inc(q["written"][s], 16)
            rolled(sp, CN, body, n)

        def hop_act(act, h, n):
            q, k = hs, h % (HOPS - 1)
            idx = srcc if k == 0 else ridx

            def stage(it, s):
                col = it * (2 * CB) + s * CB
                nc.scalar.copy(istage[s][:, 0:CB], idx[:, bass.ds(col, CB)]).then_inc(q["staged"][s], 1)
                nc.scalar.copy(fj(m_[s], CB + 1),
                               over_f(maskc[:, bass.ds(it * (2 * (CB + 1)) + s * (CB + 1), CB + 1)])
                               ).then_inc(q["masked"][s], 1)

            def body(it):
                for s in range(2):
                    act.wait_ge(q["scanned"], so_far(h, n, it, 2, s + 1))
                    if not first(it):
                        act.wait_ge(q["written"][s], so_far(h, n, it, 16, 0))
                    nc.scalar.copy(jf(r_[s], CB), fj(s_[s], CB + 1)[:, :, 1:CB + 1]).then_inc(q["rowed"], 1)
                    stage(it + 1, s)
            for s in range(2):
                stage(0, s)
            rolled(act, CN, body, n)

        def hop_dve(dve, h, n):
            q, k = hs, h % (HOPS - 1)
            wt = w1 if k == 0 else w2
            ch = hop_chain[0]
            nc.vector.memset(s_[1][:, 0:D * (CB + 1)], 0.0).then_inc(q["carried"], 1)
            dve.wait_ge(q["carried"], 2 * h + 1)

            def body(it):
                ch.begin(it, h, n)
                for s in range(2):
                    dve.wait_ge(q["gathered"][s], so_far(h, n, it, 16 * CB, 16 * CB))
                    ch.link(nc.vector.tensor_tensor(fj(v_[s], CB + 1)[:, :, 1:CB + 1], jf(g_[s], CB),
                                                    over_f(wt[:, bass.ds(it * (2 * CB) + s * CB, CB)]), ALU.mult))
                    if not (first(it) and s == 0):
                        dve.wait_ge(q["scanned"], so_far(h, n, it, 2, s))
                    ch.link(nc.vector.tensor_copy(fj(v_[s], CB + 1)[:, :, 0:1], fj(s_[1 - s], CB + 1)[:, :, CB:CB + 1]))
                    dve.wait_ge(q["masked"][s], so_far(h, n, it, 1, 1, 1))
                    nc.vector.tensor_tensor_scan(s_[s][:, 0:D * (CB + 1)], m_[s][:, 0:D * (CB + 1)],
                                                 v_[s][:, 0:D * (CB + 1)], 0.0, ALU.mult, ALU.add
                                                 ).then_inc(q["scanned"], 1)
                ch.end()
            rolled(dve, CN, body, n)
            dve.wait_ge(spread, spread_no[f"h{h}"])
            nc.vector.tensor_copy(carry[:, :], ps_c[:, 0:D]).then_inc(q["carried"], 1)

        def hop_pe(pe, h, n):
            q = hs
            pe.wait_ge(q["scanned"], n * (2 * (h + 1)))
            nc.tensor.matmul(ps_c[:, 0:D], matc[:, :], fj(s_[1], CB + 1)[:, :, CB], start=True, stop=True
                             ).then_inc(spread, 1)

        def scatter(pool, tabs, idx, data, done, it, s, j, per, round=0, turns=0):
            k = len(tabs)
            before_it = (s * per + j) // k
            if not (first(it) and before_it == 0):
                pool.wait_ge(done[j % k], so_far(round, turns, it, 2 * 16 * per // k, 16 * before_it))
                pool.sem_inc(pool_step, 1)
            pool.indirect_dma_start(out=tabs[j % k], out_offset=bass.IndirectOffsetOnAxis(ap=idx, axis=0),
                                    in_=data, in_offset=None).then_inc(done[j % k], 16)

        def hop_pool(pool, h, n):
            q, k = hs, h % (HOPS - 1)
            tab = (x if h == 0 else node_tab) if k == 0 else hop_tab[k - 1]

            def body(it):
                for s in range(2):
                    pool.wait_ge(q["staged"][s], so_far(h, n, it, 1, 1, 1))
                    pool.sem_inc(pool_step, 1)
                    for j in range(CB):
                        pool.indirect_dma_start(
                            out=g_[s][:, j * D:(j + 1) * D], out_offset=None, in_=tab,
                            in_offset=bass.IndirectOffsetOnAxis(ap=istage[s][:, j:j + 1], axis=0)
                        ).then_inc(q["gathered"][s], 16)
            rolled(pool, CN, body, n)
            for s in range(2):
                pool.wait_ge(q["written"][s], n * (16 * (h + 1)))
            pool.wait_ge(q["carried"], 2 * h + 2)
            pool.sem_inc(pool_step, 1)
            pool.indirect_dma_start(out=hop_tab[k], out_offset=bass.IndirectOffsetOnAxis(ap=ci32[:, 1:2], axis=0),
                                    in_=carry[:, :], in_offset=None, compute_op=ALU.add).then_inc(fixed, 16)
            nfix[0] += 1
            pool.wait_ge(fixed, 16 * nfix[0])

        fixed = sem("fixed")
        nfix = [0]
        pool_step = sem("pool_step")
        spread_no = {"r1": 1, "r2": 2, "r3": 3, "r4": 4}
        for c in range(2):
            for k in range(HOPS - 1):
                spread_no[f"h{c * (HOPS - 1) + k}"] = 5 + c * (HOPS + 1) + k
            spread_no[f"f{c}"] = 5 + c * (HOPS + 1) + HOPS - 1
        spread_no["l1"] = 5 + 2 * (HOPS + 1)

        def fold_sp(sp, c, n):
            q = fs

            def body(it):
                for s in range(2):
                    if not first(it):
                        sp.wait_ge(q["transposed"], so_far(c, n, it, 4, s * 2 - 2))
                    for k in range(HOPS - 1):
                        sp.dma_start(tl_[s][:, k * CB * D:(k + 1) * CB * D],
                                     hop_rows(k)[:, bass.ds(it * (2 * CB * D) + s * CB * D, CB * D)]
                                     ).then_inc(q["loaded"][s], 16)
            rolled(sp, CN, body, n)

        def fold_act(act, c, n):
            q = fs

            def stage(it, s):
                nc.scalar.copy(istage[s][:, 0:CB], ridx[:, bass.ds(it * (2 * CB) + s * CB, CB)]
                               ).then_inc(q["staged"][s], 1)
                nc.scalar.copy(fj(m_[s], CB + 1),
                               over_f(maskc[:, bass.ds(it * (2 * (CB + 1)) + s * (CB + 1), CB + 1)])
                               ).then_inc(q["masked"][s], 1)

            def body(it):
                for s in range(2):
                    act.wait_ge(q["scanned"], so_far(c, n, it, 2, s + 1))
                    stage(it + 1, s)
                    if not first(it):
                        act.wait_ge(q["transposed"], so_far(c, n, it, 4, s * 2 - 2))
                        for t in range(ST):
                            act.wait_ge(q["scattered"][t], so_far(c, n, it, 2 * PER, (s - 1) * PER))
                    nc.scalar.copy(jf(hb_[s], CB), fj(s_[s], CB + 1)[:, :, 1:CB + 1]).then_inc(q["rowed"], 1)
                    nc.scalar.copy(eidx_[s][:, 0:CB], uidx[:, bass.ds(it * (2 * CB) + s * CB, CB)]
                                   ).then_inc(q["ready"][s], 1)
                    for g in range(2):
                        act.wait_ge(q["transposed"], so_far(c, n, it, 4, s * 2 + g + 1))
                        if not (first(it) and s == 0):
                            act.wait_ge(q["mult"], so_far(c, n, it, 4, s * 2 + g - 1))
                        nc.scalar.copy(tt_[g][:, :], ps_t[g][:, 0:HOPS * P]).then_inc(q["copied"], 1)
            for s in range(2):
                stage(0, s)
            rolled(act, CN, body, n)

        def fold_pe(pe, c, n):
            q = fs

            def body(it):
                for s in range(2):
                    pe.wait_ge(q["loaded"][s], so_far(c, n, it, 16 * (HOPS - 1), 16 * (HOPS - 1)))
                    pe.wait_ge(q["rowed"], so_far(c, n, it, 2, s + 1))
                    for g in range(2):
                        if not (first(it) and s == 0):
                            pe.wait_ge(q["copied"], so_far(c, n, it, 4, s * 2 + g - 1))
                        for k in range(HOPS):
                            of = hb_[s][:, g * P:(g + 1) * P] if k == HOPS - 1 else \
                                tl_[s][:, (2 * k + g) * P:(2 * k + g + 1) * P]
                            ins = nc.tensor.transpose(ps_t[g][:, k * P:(k + 1) * P], of, ident[:, :])
                        ins.then_inc(q["transposed"], 1)
                    if not first(it):
                        pe.wait_ge(q["ready"][s], so_far(c, n, it, 2, 0))
                    for g in range(2):
                        pe.wait_ge(q["copied"], so_far(c, n, it, 4, s * 2 + g + 1))
                        for k in range(HOPS):
                            ins = nc.tensor.matmul(ps_o[s][:, g * P:(g + 1) * P], tt_[g][:, k * P:(k + 1) * P],
                                                   bd[:, (c * (HOPS + 1) + k + 1) * P:(c * (HOPS + 1) + k + 2) * P],
                                                   start=(k == 0), stop=(k == HOPS - 1))
                        ins.then_inc(q["mult"], 1)
            rolled(pe, CN, body, n)
            pe.wait_ge(q["scanned"], n * (2 * (c + 1)))
            nc.tensor.matmul(ps_c[0:D, 0:P], fj(s_[1], CB + 1)[:, :, CB], matc[:, :], start=True, stop=True
                             ).then_inc(spread, 1)
            pe.wait_ge(q["carried"], 3 * c + 2)
            w0 = (c * (HOPS + 1) + HOPS) * P
            nc.tensor.matmul(ps_b[:, 0:D], tt_[0][0:D, 0:P], bd[0:D, w0:w0 + D], start=True, stop=True
                             ).then_inc(spread, 1)

        def fold_dve(dve, c, n):
            q = fs
            ch = fold_chain[0]
            nc.vector.memset(s_[1][:, 0:D * (CB + 1)], 0.0).then_inc(q["carried"], 1)
            dve.wait_ge(q["carried"], 3 * c + 1)

            def body(it):
                ch.begin(it, c, n)
                for s in range(2):
                    dve.wait_ge(q["gathered"][s], so_far(c, n, it, 16 * CB, 16 * CB))
                    ch.link(nc.vector.tensor_tensor(fj(v_[s], CB + 1)[:, :, 1:CB + 1], jf(g_[s], CB),
                                                    over_f(w2[:, bass.ds(it * (2 * CB) + s * CB, CB)]), ALU.mult))
                    if not (first(it) and s == 0):
                        dve.wait_ge(q["scanned"], so_far(c, n, it, 2, s))
                    ch.link(nc.vector.tensor_copy(fj(v_[s], CB + 1)[:, :, 0:1], fj(s_[1 - s], CB + 1)[:, :, CB:CB + 1]))
                    dve.wait_ge(q["masked"][s], so_far(c, n, it, 1, 1, 1))
                    if not first(it):
                        dve.wait_ge(q["rowed"], so_far(c, n, it, 2, s - 1))
                    nc.vector.tensor_tensor_scan(s_[s][:, 0:D * (CB + 1)], m_[s][:, 0:D * (CB + 1)],
                                                 v_[s][:, 0:D * (CB + 1)], 0.0, ALU.mult, ALU.add
                                                 ).then_inc(q["scanned"], 1)
                    dve.wait_ge(q["mult"], so_far(c, n, it, 4, s * 2 + 2))
                    if not first(it):
                        for t in range(ST):
                            dve.wait_ge(q["scattered"][t], so_far(c, n, it, 2 * PER, (s - 1) * PER))
                    nc.vector.tensor_tensor(rows(r_[s][:, 0:CB * D]), rows(ps_o[s][:, 0:CB * D]),
                                            over_row(sdd[:, bass.ds(it * (2 * CB) + s * CB, CB)]), ALU.mult
                                            ).then_inc(q["ready"][s], 1)
                ch.end()
            rolled(dve, CN, body, n)
            dve.wait_ge(spread, spread_no[f"f{c}"])
            nc.vector.tensor_copy(tt_[0][0:D, 0:P], ps_c[0:D, 0:P]).then_inc(q["carried"], 1)
            dve.wait_ge(spread, spread_no[f"f{c}"] + 1)
            nc.vector.tensor_scalar(carry[:, :], ps_b[:, 0:D], sdh[:, 0:1], None, ALU.mult).then_inc(q["carried"], 1)

        def fold_pool(pool, c, n, n_less):
            q = fs

            def gather(s, j):
                pool.indirect_dma_start(
                    out=g_[s][:, j * D:(j + 1) * D], out_offset=None, in_=hop_tab[HOPS - 2],
                    in_offset=bass.IndirectOffsetOnAxis(ap=istage[s][:, j:j + 1], axis=0)
                ).then_inc(q["gathered"][s], 16)

            def body(it, more=True):
                for s in range(2):
                    if more:
                        pool.wait_ge(q["staged"][s], so_far(c, n, it, 1, 2, 1))
                    pool.wait_ge(q["ready"][s], so_far(c, n, it, 2, 2))
                    pool.sem_inc(pool_step, 1)
                    for j in range(CB):
                        if more:
                            gather(s, j)
                        scatter(pool, node_sum, eidx_[s][:, j:j + 1], r_[s][:, j * D:(j + 1) * D],
                                q["scattered"], it, s, j, CB, c, n)
            for s in range(2):
                pool.wait_ge(q["staged"][s], so_far(c, n, 0, 1, 1, 1))
                pool.sem_inc(pool_step, 1)
                for j in range(CB):
                    gather(s, j)
            rolled(pool, CN, body, n_less)
            body(n_less, more=False)
            for t in range(ST):
                pool.wait_ge(q["scattered"][t], n * (2 * PER * (c + 1)))
            pool.wait_ge(q["carried"], 3 * c + 3)
            pool.sem_inc(pool_step, 1)
            pool.indirect_dma_start(out=node_sum[0], out_offset=bass.IndirectOffsetOnAxis(ap=ci32[:, 3:4], axis=0),
                                    in_=carry[:, :], in_offset=None, compute_op=ALU.add).then_inc(fixed, 16)
            nfix[0] += 1
            pool.wait_ge(fixed, 16 * nfix[0])

        PARTS = [4, 4, 4, 2]

        def prod_pe(pe, q, have, c, last_apart=0):
            def body(it):
                for s in range(2):
                    rows_in = have(it, s)
                    at = 0
                    for i, m in enumerate(PARTS):
                        no = it * 8 + s * 4 + i
                        if not (first(it) and s == 0 and i < 2):
                            pe.wait_ge(q["cp"], no - 1)
                        for g in range(m):
                            ins = nc.tensor.transpose(ps_t[i % 2][:, g * P:(g + 1) * P],
                                                      rows_in(at + g * P, P), ident[:, :])
                        ins.then_inc(q["tr"], 1)
                        at += m * P
                        pe.wait_ge(q["cp"], no + 1)
                        if not (first(it) and s == 0 and i < 2):
                            pe.wait_ge(q["ev"], no - 1)
                        for g in range(m):
                            nc.tensor.matmul(ps_o[i % 2][:, g * P:(g + 1) * P], xt[i % 2][:, g * P:(g + 1) * P],
                                             bd[:, c * (HOPS + 1) * P:(c * (HOPS + 1) + 1) * P],
                                             start=True, stop=False)
                            ins = nc.tensor.matmul(ps_o[i % 2][:, g * P:(g + 1) * P], ones[0:1, 0:P],
                                                   brow[0:1, c * 512:c * 512 + P], start=False, stop=True)
                        ins.then_inc(q["mm"], 1)
            rolled(pe, ITS, body, last_apart=last_apart)

        def prod_act(act, q, it, s):
            for i, m in enumerate(PARTS):
                no = it * 8 + s * 4 + i
                act.wait_ge(q["tr"], no + 1)
                if not (first(it) and s == 0 and i < 2):
                    act.wait_ge(q["mm"], no - 1)
                nc.scalar.copy(xt[i % 2][:, 0:m * P], ps_t[i % 2][:, 0:m * P]).then_inc(q["cp"], 1)

        def x_load(eng, it, s, to, done):
            if isinstance(it, int) and it == ITS - 1 and s == 1:
                b = NBLK - 1
                n0 = b * P * NB
                eng.dma_start(to[0:LASTP, :], x[n0:n0 + LASTP * NB, :].rearrange("(p c) f -> p (c f)", c=NB)
                              ).then_inc(done, 16)
                eng.dma_start(to[LASTP:LASTP + 1, 0:LASTC * D],
                              x[n0 + LASTP * NB:N, :].rearrange("(p c) f -> p (c f)", p=1)).then_inc(done, 16)
            else:
                eng.dma_start(to, node_rows(x, it * 2 + s)).then_inc(done, 16)

        def dense_sp(sp, i):
            q = dense[i]

            def load(it, s):
                if not first(it):
                    sp.wait_ge(q["add"], (it - 1) * 2 + s + 1)
                tabs = agg_sum if i == 2 else node_sum
                sp.dma_start(ub[s], node_rows(tabs[0], it * 2 + s)).then_inc(q["ul"][s], 16)
                if i == 1 and not first(it):
                    sp.wait_ge(q["done"], (it - 1) * 2 + s + 1)
                sp.dma_start(cb[s] if i == 1 else xb[s], node_rows(tabs[1], it * 2 + s)).then_inc(q["ul"][s], 16)
                if i == 1:
                    x_load(sp, it, s, xb[s], bs["xl"][s])
                if i == 0:
                    for k, v in enumerate((gamma, beta)):
                        to = gb[s][:, k * NB:(k + 1) * NB]
                        if isinstance(it, int) and it == ITS - 1 and s == 1:
                            n0 = (NBLK - 1) * P * NB
                            sp.dma_start(to[0:LASTP, :], v[n0:n0 + LASTP * NB].rearrange("(p c) -> p c", c=NB)
                                         ).then_inc(gb_in[s], 16)
                            sp.dma_start(to[LASTP:LASTP + 1, 0:LASTC],
                                         v[n0 + LASTP * NB:N].rearrange("(p c) -> p c", p=1)).then_inc(gb_in[s], 16)
                        else:
                            sp.dma_start(to, v[bass.ds((it * 2 + s) * (P * NB), P * NB)].rearrange("(p c) -> p c", p=P)
                                         ).then_inc(gb_in[s], 16)

            def store(it, s):
                b = it * 2 + s
                sp.wait_ge(q["done"], b + 1)
                if i < 2:
                    sp.dma_start(node_rows(node_tab, b), nd[:, bass.ds(b * W, W)]).then_inc(q["stored"][s], 16)
                elif isinstance(it, int) and it == ITS - 1 and s == 1:
                    n0 = b * P * NB
                    sp.dma_start(out[n0:n0 + LASTP * NB, :].rearrange("(p c) f -> p (c f)", c=NB),
                                 cb[s][0:LASTP, :]).then_inc(q["stored"][s], 16)
                    sp.dma_start(out[n0 + LASTP * NB:N, :].rearrange("(p c) f -> p (c f)", p=1),
                                 cb[s][LASTP:LASTP + 1, 0:LASTC * D]).then_inc(q["stored"][s], 16)
                else:
                    sp.dma_start(node_rows(out, b), cb[s]).then_inc(q["stored"][s], 16)

            def body(it):
                for s in range(2):
                    store(it, s)
                    if not (isinstance(it, int) and it == ITS - 1):
                        load(it + 1, s)
            for s in range(2):
                load(0, s)
            rolled(sp, ITS, body, last_apart=2)
            sp.wait_ge(q["stored"][0], 16 * ITS)
            sp.wait_ge(q["stored"][1], 16 * (ITS + (i == 2)))

        def dense_act(act, i):
            q = dense[i]

            def body(it):
                if i == 1:
                    for s in range(2):
                        if not first(it):
                            act.wait_ge(q["done"], it * 2 + s - 1)
                        nc.scalar.copy(sq[s], nd[:, bass.ds((it * 2 + s) * W, W)]).then_inc(bs["zs"][s], 1)
                        prod_act(act, bs, it, s)
                for s in range(2):
                    b = it * 2 + s
                    act.wait_ge(q["cen"], b + 1)
                    nc.scalar.activation(sq[s], cb[s], ACT.Square).then_inc(q["sq"], 1)
                for s in range(2):
                    act.wait_ge(q["var"], it * 2 + s + 1)
                    nc.scalar.activation(st[s][:, NB:2 * NB], st[s][:, NB:2 * NB], ACT.Sqrt).then_inc(q["root"], 1)
            rolled(act, ITS, body)

        def dense_pool(pool, i):
            q = dense[i]

            def body(it):
                for s in range(2):
                    pool.wait_ge(q["ul"][s], it * 32 + 32)
                    nc.gpsimd.tensor_tensor(ub[s], ub[s], cb[s] if i == 1 else xb[s], ALU.add
                                            ).then_inc(q["both"], 1)
            rolled(pool, ITS, body)

        def dense_dve(dve, i):
            q = dense[i]
            ch = Chain(dve, q["chain"])

            def body(it):
                ch.begin(it)
                for s in range(2):
                    b = it * 2 + s
                    blk = nd[:, bass.ds(b * W, W)]
                    dve.wait_ge(q["both"], b + 1)
                    if i == 0:
                        ch.link(nc.vector.tensor_tensor(cb[s], blk, ub[s], ALU.add))
                    elif i == 1:
                        o = 0
                        for p, m in enumerate(PARTS):
                            no = it * 8 + s * 4 + p
                            dve.wait_ge(bs["mm"], no + 1)
                            ins = nc.vector.tensor_tensor(ub[s][:, o:o + m * P], ub[s][:, o:o + m * P],
                                                          ps_o[p % 2][:, 0:m * P], ALU.add)
                            ins.then_inc(bs["ev"], 1)
                            o += m * P
                        dve.wait_ge(bs["ev"], it * 8 + s * 4 + 4)
                        ch.link(nc.vector.tensor_tensor(rows(ub[s]), rows(ub[s]),
                                                        over_row(nvs[:, bass.ds(b * NB, NB)]), ALU.mult))
                        if isinstance(it, int) and it == ITS - 1 and s == 1:
                            dve.wait_ge(bs["xl"][s], ITS * 16 + 16)
                        else:
                            dve.wait_ge(bs["xl"][s], it * 16 + 16)
                        ch.link(nc.vector.tensor_tensor(cb[s], ub[s], xb[s], ALU.add))
                    else:
                        if not first(it):
                            dve.wait_ge(q["stored"][s], it * 16)
                        ch.link(nc.vector.scalar_tensor_tensor(cb[s], blk, 2.0, ub[s], ALU.mult, ALU.add))
                    ch.link(nc.vector.tensor_reduce(st[s][:, 0:NB], rows(cb[s]), AX.X, ALU.add))
                    ch.link(nc.vector.tensor_scalar(st[s][:, 0:NB], st[s][:, 0:NB], 1.0 / D, None, ALU.mult))
                    ch.link(nc.vector.tensor_tensor(rows(cb[s]), rows(cb[s]), over_row(st[s][:, 0:NB]), ALU.subtract))
                    dve.sem_inc(q["cen"], 1)
                    if i > 0:
                        dve.sem_inc(q["add"], 1)
                for s in range(2):
                    b = it * 2 + s
                    dve.wait_ge(q["sq"], b + 1)
                    ch.link(nc.vector.tensor_reduce(st[s][:, NB:2 * NB], rows(sq[s]), AX.X, ALU.add))
                    nc.vector.tensor_scalar(st[s][:, NB:2 * NB], st[s][:, NB:2 * NB], 1.0 / D, EPS,
                                            ALU.mult, ALU.add).then_inc(q["var"], 1)
                for s in range(2):
                    b = it * 2 + s
                    dve.wait_ge(q["root"], b + 1)
                    ch.link(nc.vector.reciprocal(st[s][:, NB:2 * NB], st[s][:, NB:2 * NB]))
                    if i == 0:
                        dve.wait_ge(gb_in[s], it * 32 + 32 + (32 if isinstance(it, int) and it == ITS - 1 and s else 0))
                        ch.link(nc.vector.tensor_tensor(st[s][:, NB:2 * NB], st[s][:, NB:2 * NB], gb[s][:, 0:NB],
                                                        ALU.mult))
                    to = nd[:, bass.ds(b * W, W)] if i == 1 else cb[s]
                    ch.link(nc.vector.tensor_tensor(rows(to), rows(cb[s]), over_row(st[s][:, NB:2 * NB]), ALU.mult))
                    if i == 0:
                        ch.link(nc.vector.tensor_tensor(rows(cb[s]), rows(cb[s]), over_row(gb[s][:, NB:2 * NB]),
                                                        ALU.add))
                        ch.link(nc.vector.scalar_tensor_tensor(nd[:, bass.ds(b * W, W)], cb[s], SLOPE, cb[s],
                                                               ALU.mult, ALU.max))
                        dve.sem_inc(q["add"], 1)
                    dve.sem_inc(q["done"], 1)
                ch.end()
            rolled(dve, ITS, body, last_apart=int(i < 2))

        @block.sync
        def _(sp):
            for a, b, r in ((e_src, src, 16), (e_dst, dst, 16), (e_w, weight, 16)):
                sp.dma_start(b_split(a[0:E], r), b_split(b, r)).then_inc(copied, 16)
            sp.wait_ge(zeroed, 2)
            pad = EP - E
            sp.dma_start(e_src[E:EP].rearrange("(a b) -> a b", a=1), zeros[0:1, 0:pad].bitcast(I32)).then_inc(copied, 16)
            sp.dma_start(e_dst[E:EP].rearrange("(a b) -> a b", a=1), padi[:, :]).then_inc(copied, 16)
            sp.dma_start(e_w[E:EP].rearrange("(a b) -> a b", a=1), zeros[0:1, 0:pad]).then_inc(copied, 16)
            for t in range(LT):
                sp.dma_start(node_lasts[t].rearrange("(p a) b -> p (a b)", p=P), zeros[:, :]).then_inc(tabs0, 16)
            sp.dma_start(edge_info[0:1, :], zeros[0:1, 0:2]).then_inc(tabs0, 16)
            for k in range(HOPS - 1):
                sp.dma_start(hop_tab[k][0:1, :], zeros[0:1, 0:D]).then_inc(tabs0, 16)
                sp.dma_start(hop_tab[k][1 + TROWS:, :], zeros[:, 0:D]).then_inc(tabs0, 16)
            sp.wait_ge(copied, 16 * 6)
            sp.dma_start(e_i[:, 0, :], ev(e_src)).then_inc(loaded, 16)
            sp.dma_start(e_i[:, 1, :], ev(e_dst)).then_inc(loaded, 16)
            sp.dma_start(w_e[:, :], ev(e_w)).then_inc(loaded, 16)
            sp.wait_ge(tabs0, 16 * (LT + 1 + 2 * (HOPS - 1)))
            phase_end(sp, "sp")
            def body(it):
                for s in range(2):
                    if not first(it):
                        sp.wait_ge(a0["tr"], (it * 2 + s - 1) * 4)
                    x_load(sp, it, s, xb[s], a0["xl"][s])
            rolled(sp, ITS, body, last_apart=1)
            phase_end(sp, "sp")
            for t in range(LT):
                sp.dma_start(lasts[t], node_lasts[t].rearrange("(p a) b -> p (a b)", p=P)).then_inc(lasts_in, 16)
            sp.wait_ge(lasts_sum, LT)
            sp.dma_start(node_last.rearrange("(p a) b -> p (a b)", p=P), lasts[0]).then_inc(lasts_in, 16)
            sp.wait_ge(lasts_in, 16 * (LT + 1))
            phase_end(sp, "sp")
            phase_end(sp, "sp")
            phase_end(sp, "sp")
            sp.dma_start(edge_info[1:1 + EP, :].rearrange("(p j) b -> p (j b)", p=P),
                         ei.rearrange("p j b -> p (j b)")).then_inc(info_out, 16)
            sp.wait_ge(info_out, 16)
            phase_end(sp, "sp")
            n = sp.value_load(n_it[0:1, 0:1], min_val=2, max_val=CN)
            phase_end(sp, "sp")
            phase_end(sp, "sp")
            for c in range(2):
                for k in range(HOPS - 1):
                    hop_sp(sp, c * (HOPS - 1) + k, n)
                    phase_end(sp, "sp")
                fold_sp(sp, c, n)
                phase_end(sp, "sp")
                dense_sp(sp, c)
                phase_end(sp, "sp")

            def body(it):
                for s in range(2):
                    if not first(it):
                        sp.wait_ge(ls["scanned"], it * 2 + s - 1)
                    sp.dma_start(a_[s], attr_v[:, bass.ds((it * 2 + s) * EB * D, EB * D)]).then_inc(ls["attr"][s], 16)
            rolled(sp, ITS, body)
            phase_end(sp, "sp")
            dense_sp(sp, 2)
            phase_end(sp, "sp")

        @block.gpsimd
        def _(pool):
            pool.memset(ident[:, :], 0.0).then_inc(consts, 1)
            pool.memset(before[:, :], 1.0).then_inc(consts, 1)
            pool.memset(after[:, :], 1.0).then_inc(consts, 1)
            pool.wait_ge(consts, 3)
            pool.affine_select(out=ident[:, :], in_=ident[:, :], compare_op=ALU.not_equal, fill=1.0, base=0,
                               pattern=[[-1, P]], channel_multiplier=1)
            pool.affine_select(out=before[:, :], in_=before[:, :], compare_op=ALU.is_gt, fill=0.0, base=0,
                               pattern=[[1, P]], channel_multiplier=-1)
            pool.affine_select(out=after[:, :], in_=after[:, :], compare_op=ALU.is_gt, fill=0.0, base=0,
                               pattern=[[-1, P]], channel_multiplier=1)
            pool.iota(col_i[:, :], [[1, JC]], base=1, channel_multiplier=0, allow_small_or_imprecise_dtypes=True)
            pool.iota(edge_no[:, :], [[1, J]], base=1, channel_multiplier=J, allow_small_or_imprecise_dtypes=True)
            for i, (b, m) in enumerate(((N, 1), (1 + TROWS, 1), (0, JC), (0, J))):
                pool.iota(part_c[:, i:i + 1], [[0, 1]], base=b, channel_multiplier=m,
                          allow_small_or_imprecise_dtypes=True)
            pool.drain().then_inc(consts_ready, 1)
            phase_end(pool, "pool")

            def body(it):
                for s in range(2):
                    pool.wait_ge(rs["staged"][s], it * 2 + 2)
                    pool.sem_inc(pool_step, 1)
                    for j in range(EB):
                        scatter(pool, node_lasts, istage[s][:, j:j + 1], st[s][:, j:j + 1],
                                rs["scattered"], it, s, j, EB)
            rolled(pool, ITS, body)
            for t in range(LT):
                pool.wait_ge(rs["scattered"][t], ITS * 2 * EB // LT * 16)
            phase_end(pool, "pool")
            phase_end(pool, "pool")

            def body(it):
                for s in range(2):
                    pool.wait_ge(rg["staged"][s], it + 1)
                    pool.sem_inc(pool_step, 1)
                    for j in range(EB):
                        pool.indirect_dma_start(
                            out=st[s][:, j:j + 1], out_offset=None, in_=node_last,
                            in_offset=bass.IndirectOffsetOnAxis(ap=istage[s][:, j:j + 1], axis=0)
                        ).then_inc(rg["gathered"][s], 16)
            rolled(pool, ITS, body)
            phase_end(pool, "pool")
            phase_end(pool, "pool")
            phase_end(pool, "pool")
            n = pool.value_load(n_it[0:1, 0:1], min_val=2, max_val=CN)
            n_less = pool.value_load(n_it[0:1, 1:2], min_val=1, max_val=CN - 1)

            def body(it):
                for s in range(2):
                    pool.wait_ge(eg_s["staged"][s], it + 1)
                    pool.sem_inc(pool_step, 1)
                    for j in range(CB):
                        pool.indirect_dma_start(
                            out=st[s][:, 2 * j:2 * j + 2], out_offset=None, in_=edge_info,
                            in_offset=bass.IndirectOffsetOnAxis(ap=istage[s][:, j:j + 1], axis=0)
                        ).then_inc(eg_s["gathered"][s], 16)
            rolled(pool, CN, body, n)
            phase_end(pool, "pool")
            phase_end(pool, "pool")
            for c in range(2):
                for k in range(HOPS - 1):
                    hop_pool(pool, c * (HOPS - 1) + k, n)
                    phase_end(pool, "pool")
                fold_pool(pool, c, n, n_less)
                phase_end(pool, "pool")
                dense_pool(pool, c)
                phase_end(pool, "pool")

            def l_gather(s, j):
                pool.indirect_dma_start(
                    out=g_[s][:, j * D:(j + 1) * D], out_offset=None, in_=node_tab,
                    in_offset=bass.IndirectOffsetOnAxis(ap=istage[s][:, j:j + 1], axis=0)
                ).then_inc(ls["gathered"][s], 16)

            pool.wait_ge(ls["staged"][0], 1)
            for j in range(EB):
                l_gather(0, j)

            def body(it):
                for s in range(2):
                    more = not (isinstance(it, int) and it == ITS - 1 and s == 1)
                    if more:
                        pool.wait_ge(ls["staged"][1 - s], it + s + 1)
                        pool.sem_inc(pool_step, 1)
                    for j in range(EB + LEAD):
                        if more and j < EB:
                            l_gather(1 - s, j)
                        if j == LEAD:
                            pool.wait_ge(ls["ready"][s], it * 2 + 2)
                            pool.sem_inc(pool_step, 1)
                        if j >= LEAD:
                            scatter(pool, agg_sum, eidx_[s][:, j - LEAD:j - LEAD + 1],
                                    r_[s][:, (j - LEAD) * D:(j - LEAD + 1) * D], ls["scattered"], it, s, j - LEAD, EB)
            rolled(pool, ITS, body, last_apart=1)
            for t in range(ST):
                pool.wait_ge(ls["scattered"][t], ITS * 2 * EB // ST * 16)
            pool.wait_ge(ls["carried"], 1)
            pool.indirect_dma_start(out=agg_sum[0], out_offset=bass.IndirectOffsetOnAxis(ap=ci32[:, 0:1], axis=0),
                                    in_=carry[:, :], in_offset=None, compute_op=ALU.add).then_inc(fixed, 16)
            nfix[0] += 1
            pool.wait_ge(fixed, 16 * nfix[0])
            phase_end(pool, "pool")
            dense_pool(pool, 2)
            phase_end(pool, "pool")

        @block.scalar
        def _(act):
            act.wait_ge(bd0, 2)
            for l, (w, b) in enumerate(((W0, b0), (W1, b1))):
                for k in range(HOPS + 1):
                    for g in range(GC):
                        c0 = (l * (HOPS + 1) + k) * P + g * D
                        act.dma_start(bd[g * D:(g + 1) * D, c0:c0 + D], w[k, :, :]).then_inc(wts, 16)
                for g in range(512 // D):
                    act.dma_start(brow[0:1, l * 512 + g * D:l * 512 + (g + 1) * D],
                                  b.rearrange("(a f) -> a f", a=1)).then_inc(wts, 16)
            nb1 = (NBLK - 1) * NB
            act.dma_start(nvs[:, 0:nb1].rearrange("p (b c) -> p b c", c=NB),
                          nv[0:nb1 * P].rearrange("(b p c) -> p b c", p=P, c=NB)).then_inc(wts, 16)
            n0 = nb1 * P
            act.dma_start(nvs[0:LASTP, nb1:], nv[n0:n0 + LASTP * NB].rearrange("(p c) -> p c", c=NB)).then_inc(wts, 16)
            act.dma_start(nvs[LASTP:LASTP + 1, nb1:nb1 + LASTC],
                          nv[n0 + LASTP * NB:N].rearrange("(p c) -> p c", p=1)).then_inc(wts, 16)
            act.wait_ge(wts, 16 * (2 * (HOPS + 1) * GC + 2 * 512 // D + 3))
            phase_end(act, "act")
            for t in node_sum + agg_sum:
                act.dma_start(t.rearrange("(p a) f -> p (a f)", p=P).rearrange("p (a b) -> p a b", a=D),
                              zeros[:, :].unsqueeze(1).to_broadcast([P, D, (NP + P) // P])).then_inc(big0, 16)
            for k in range(HOPS - 1):
                act.dma_start(hop_rows(k).rearrange("p (a b) -> p a b", a=HT),
                              zeros[:, 0:JC * D // HT].unsqueeze(1).to_broadcast([P, HT, JC * D // HT])
                              ).then_inc(big0, 16)
            act.dma_start(e_attr[0:E, :].rearrange("(a b) f -> a (b f)", a=16),
                         attr.rearrange("(a b) f -> a (b f)", a=16)).then_inc(big0, 16)
            act.dma_start(e_attr[E:EP, :].rearrange("(p a) f -> p (a f)", a=2), zeros[0:(EP - E) // 2, 0:2 * D]
                          ).then_inc(big0, 16)

            def body(it):
                for s in range(2):
                    if not first(it):
                        for t in range(LT):
                            act.wait_ge(rs["scattered"][t], (it * 2 + s - 1) * (EB // LT * 16))
                    nc.scalar.copy(istage[s][:, :], sidx[:, bass.ds((it * 2 + s) * EB, EB)]).then_inc(rs["staged"][s], 1)
                    nc.scalar.copy(st[s][:, 0:EB], edge_no[:, bass.ds((it * 2 + s) * EB, EB)]
                                   ).then_inc(rs["staged"][s], 1)
                    prod_act(act, a0, it, s)
            rolled(act, ITS, body)
            phase_end(act, "act")
            phase_end(act, "act")

            def stage(it, s):
                nc.scalar.copy(istage[s][:, :], e_i[:, 0, bass.ds((it * 2 + s) * EB, EB)]).then_inc(rg["staged"][s], 1)

            def body(it):
                for s in range(2):
                    act.wait_ge(rg["gathered"][s], it * (16 * EB) + 16 * EB)
                    nc.scalar.copy(rv[:, bass.ds((it * 2 + s) * EB, EB)], st[s][:, 0:EB]).then_inc(act_own, 1)
                    act.wait_ge(act_own, it * 2 + s + 1)
                    if not (isinstance(it, int) and it == ITS - 1):
                        stage(it + 1, s)
            for s in range(2):
                stage(0, s)
            rolled(act, ITS, body, last_apart=1)
            phase_end(act, "act")
            act.wait_ge(root_in, 1)
            nc.scalar.activation(sdd[:, :], sdd[:, :], ACT.Sqrt).then_inc(root_out, 1)
            phase_end(act, "act")
            phase_end(act, "act")
            n = act.value_load(n_it[0:1, 0:1], min_val=2, max_val=CN)

            def stage2(it, s):
                nc.scalar.copy(istage[s][:, 0:CB], gidx[:, bass.ds((it * 2 + s) * CB, CB)]).then_inc(eg_s["staged"][s], 1)

            def body(it):
                for s in range(2):
                    act.wait_ge(eg_s["gathered"][s], it * (16 * CB) + 16 * CB)
                    nc.scalar.copy(eg[:, bass.ds((it * 2 + s) * CB, CB), :],
                                   st[s][:, 0:2 * CB].rearrange("p (j b) -> p j b", b=2)).then_inc(act_own, 1)
                    act.wait_ge(act_own, it * 2 + s + 1 + NBLK)
                    stage2(it + 1, s)
            for s in range(2):
                stage2(0, s)
            rolled(act, CN, body, n)
            phase_end(act, "act")
            act.wait_ge(root_in, 2)
            nc.scalar.activation(live[:, :], live[:, :], ACT.Sqrt).then_inc(root_out, 1)
            act.wait_ge(big0, 16 * (2 * ST + HOPS - 1 + 2))
            phase_end(act, "act")
            for c in range(2):
                for k in range(HOPS - 1):
                    hop_act(act, c * (HOPS - 1) + k, n)
                    phase_end(act, "act")
                fold_act(act, c, n)
                phase_end(act, "act")
                dense_act(act, c)
                phase_end(act, "act")

            def stage3(it, s):
                nc.scalar.copy(istage[s][:, :], e_i[:, 0, bass.ds((it * 2 + s) * EB, EB)]).then_inc(ls["staged"][s], 1)
                nc.scalar.copy(fj(m_[s], EB + 1),
                               over_f(maske[:, bass.ds((it * 2 + s) * (EB + 1), EB + 1)])).then_inc(ls["masked"][s], 1)

            def body(it):
                for s in range(2):
                    act.wait_ge(ls["scanned"], it * 2 + s + 1)
                    if not first(it):
                        for t in range(ST):
                            act.wait_ge(ls["scattered"][t], (it * 2 + s - 1) * (16 * EB // ST))
                    nc.scalar.copy(eidx_[s][:, :], sidx[:, bass.ds((it * 2 + s) * EB, EB)]).then_inc(ls["ready"][s], 1)
                    if not (isinstance(it, int) and it == ITS - 1):
                        stage3(it + 1, s)
            for s in range(2):
                stage3(0, s)
            rolled(act, ITS, body, last_apart=1)
            phase_end(act, "act")
            dense_act(act, 2)
            phase_end(act, "act")

        @block.tensor
        def _(pe):
            pe.wait_ge(consts_ready, 1)
            pe.wait_ge(cols_ready, 1)
            for i in range(2):
                ins = nc.tensor.matmul(ps_b[:, i * P:(i + 1) * P], lb[:, i * P:(i + 1) * P], ident[:, :],
                                       start=True, stop=True)
            ins.then_inc(spread, 1)
            pe.wait_ge(cols_ready, 2)
            nc.tensor.matmul(ps_c[:, 0:2], mat[:, :], sm[:, 2:4], start=True, stop=True).then_inc(spread, 1)
            pe.wait_ge(cols_ready, 3)
            nc.tensor.matmul(ps_c[:, 2:3], mat2[:, :], sm[:, 10:11], start=True, stop=True).then_inc(spread, 1)
            phase_end(pe, "pe")

            def have(it, s):
                if isinstance(it, int) and it == ITS - 1 and s == 1:
                    pe.wait_ge(a0["xl"][s], ITS * 16 + 16)
                else:
                    pe.wait_ge(a0["xl"][s], it * 16 + 16)
                return lambda o, m: xb[s][:, o:o + m]
            prod_pe(pe, a0, have, 0, last_apart=1)
            phase_end(pe, "pe")
            phase_end(pe, "pe")
            phase_end(pe, "pe")
            pe.wait_ge(cols_ready, 4)
            for i in range(4):
                ins = nc.tensor.matmul(ps_b[:, i * P:(i + 1) * P], lb[:, i * P:(i + 1) * P], ident[:, :],
                                       start=True, stop=True)
            ins.then_inc(spread, 1)
            phase_end(pe, "pe")
            phase_end(pe, "pe")
            n = pe.value_load(n_it[0:1, 0:1], min_val=2, max_val=CN)
            phase_end(pe, "pe")
            phase_end(pe, "pe")
            for c in range(2):
                for k in range(HOPS - 1):
                    hop_pe(pe, c * (HOPS - 1) + k, n)
                    phase_end(pe, "pe")
                fold_pe(pe, c, n)
                phase_end(pe, "pe")
                if c == 1:
                    def have(it, s):
                        pe.wait_ge(bs["zs"][s], it + 1)
                        return lambda o, m: sq[s][:, o:o + m]
                    prod_pe(pe, bs, have, 1)
                phase_end(pe, "pe")
            pe.wait_ge(ls["scanned"], NBLK)
            nc.tensor.matmul(ps_c[:, 0:D], mat[:, :], fj(s_[1], EB + 1)[:, :, EB], start=True, stop=True
                             ).then_inc(spread, 1)
            phase_end(pe, "pe")
            phase_end(pe, "pe")

        @block.vector
        def _(dve):
            ch = Chain(dve, "dve_chain")
            V = nc.vector

            def tt(o, a, b, op):
                ch.link(V.tensor_tensor(o, a, b, op))

            def ts(o, a, s1, s2, o1, o2=None):
                ch.link(V.tensor_scalar(o, a, s1, s2, o1, o2) if o2 is not None else V.tensor_scalar(o, a, s1, s2, o1))

            def cp(o, a):
                ch.link(V.tensor_copy(o, a))

            def red(o, a, op=ALU.add):
                ch.link(V.tensor_reduce(o, a, AX.X, op))

            def rsqrt0(o, a, tmp, no):
                ts(tmp, a, 0.0, None, ALU.is_gt)
                V.tensor_scalar(o, a, 1.2e-38, None, ALU.max).then_inc(root_in, 1)
                dve.wait_ge(root_out, no)
                ch.link(V.reciprocal(o, o))
                tt(o, o, tmp, ALU.mult)

            head_c = pay[:, 0, :]

            def c_(i):
                return sm[:, i:i + 1]
            FIRST, LAST, PD, PC, CD, CC, CONT, HV, CF, T0, DEGEND, RCH, INITR = range(13)
            POS, FC, LC, CNT, CARP, CONTC, HVC, CFC = range(16, 24)

            V.memset(zeros[:, :], 0.0).then_inc(zeroed, 1)
            V.memset(padi[:, :], int(PADV)).then_inc(zeroed, 1)
            V.memset(ones[:, :], 1.0)
            V.memset(bd[:, :], 0.0).then_inc(bd0, 1)
            V.memset(nvs[:, :], 0.0).then_inc(bd0, 1)
            for t in (gidx, srcc, ridx, uidx):
                V.memset(t[:, JC:JX], 0)
            V.memset(w1[:, JC:JX], 0.0)
            V.memset(w2[:, JC:JX], 0.0)
            V.memset(eg[:, :, :], 0.0)
            V.memset(maskc[:, :], 0.0)
            V.memset(maske[:, :], 0.0)
            ch.link(V.memset(same[:, 0:1], 1.0))
            dve.wait_ge(loaded, 48)
            dve.wait_ge(consts_ready, 1)
            cp(d_e[:, :], e_i[:, 1, :])
            tt(same[:, 1:J], d_e[:, 1:J], d_e[:, 0:J - 1], ALU.is_equal)
            cp(c_(FIRST), d_e[:, 0:1])
            cp(c_(LAST), d_e[:, J - 1:J])
            cp(lb[:, 0:P], c_(FIRST).to_broadcast([P, P]))
            V.tensor_copy(lb[:, P:2 * P], c_(LAST).to_broadcast([P, P])).then_inc(cols_ready, 1)
            cp(maske[:, 0:(J // EB) * (EB + 1)].rearrange("p (b j) -> p b j", j=EB + 1)[:, :, 1:EB + 1],
               same[:, :].rearrange("p (b j) -> p b j", j=EB))
            ch.link(V.tensor_tensor_scan(deg[:, :], same[:, :], w_e[:, :], 0.0, ALU.mult, ALU.add))
            ch.link(V.tensor_tensor_scan(cnt[:, :], same[:, :], ones[:, :], 0.0, ALU.mult, ALU.add))
            cp(c_(PD), deg[:, J - 1:J])
            cp(c_(PC), cnt[:, J - 1:J])
            dve.wait_ge(spread, spread_no["r1"])
            ch.link(V.scalar_tensor_tensor(mat[:, :], ps_b[:, 0:P], c_(LAST), before[:, :], ALU.is_equal, ALU.mult))
            V.scalar_tensor_tensor(mat2[:, :], ps_b[:, P:2 * P], c_(FIRST), after[:, :], ALU.is_equal, ALU.mult
                                   ).then_inc(cols_ready, 1)
            dve.wait_ge(cols_ready, 2)
            red(c_(CONT), mat[:, :])
            ts(c_(CONT), c_(CONT), 0.5, None, ALU.is_gt)
            ch.link(V.memset(last[:, J - 1:J], 1.0))
            tt(last[:, 0:J - 1], d_e[:, 0:J - 1], d_e[:, 1:J], ALU.not_equal)
            ts(t_e[:, 0:J], d_e[:, :], c_(LAST), c_(CONT), ALU.is_equal, ALU.mult)
            ts(t_e[:, 0:J], t_e[:, 0:J], -1.0, 1.0, ALU.mult, ALU.add)
            tt(last[:, :], last[:, :], t_e[:, 0:J], ALU.mult)
            ts(t_e[:, 0:J], d_e[:, :], float(N), None, ALU.is_lt)
            tt(last[:, :], last[:, :], t_e[:, 0:J], ALU.mult)
            ts(head[:, :], d_e[:, :], c_(FIRST), None, ALU.is_equal)
            dve.wait_ge(spread, spread_no["r2"])
            cp(sm[:, CD:CD + 2], ps_c[:, 0:2])
            ch.link(V.tensor_tensor_scan(deg[:, :], same[:, :], w_e[:, :], c_(CD), ALU.mult, ALU.add))
            ch.link(V.tensor_tensor_scan(cnt[:, :], same[:, :], ones[:, :], c_(CC), ALU.mult, ALU.add))
            ts(rcnt[:, :], cnt[:, :], 1.0, None, ALU.max)
            ch.link(V.reciprocal(rcnt[:, :], rcnt[:, :]))
            tt(rcnt[:, :], rcnt[:, :], last[:, :], ALU.mult)
            tt(head[:, :], head[:, :], last[:, :], ALU.mult)
            red(c_(HV), head[:, :])
            tt(t_e[:, 0:J], head[:, :], deg[:, :], ALU.mult)
            red(c_(DEGEND), t_e[:, 0:J])
            tt(t_e[:, 0:J], head[:, :], rcnt[:, :], ALU.mult)
            red(c_(RCH), t_e[:, 0:J])
            dve.sem_inc(cols_ready, 1)
            tt(c_(T0), c_(FIRST), part_c[:, 0:1], ALU.subtract)
            tt(c_(T0), c_(T0), c_(HV), ALU.mult)
            tt(c_(T0), c_(T0), part_c[:, 0:1], ALU.add)
            cp(ci32[:, 0:1], c_(T0))
            ts(t_e[:, 0:J], d_e[:, :], part_c[:, 0:1], None, ALU.subtract)
            tt(t_e[:, 0:J], t_e[:, 0:J], last[:, :], ALU.mult)
            ts(t_e[:, 0:J], t_e[:, 0:J], part_c[:, 0:1], None, ALU.add)
            cp(sidx[:, :], t_e[:, 0:J])
            dve.wait_ge(spread, spread_no["r3"])
            cp(c_(INITR), ps_c[:, 2:3])
            tt(t_e[:, 0:J], last[:, :], deg[:, :], ALU.mult)
            ts(t_f[:, 0:J], last[:, :], -1.0, 1.0, ALU.mult, ALU.add)
            ch.link(V.tensor_tensor_scan(ddst[:, ::-1], t_f[:, 0:J][:, ::-1], t_e[:, 0:J][:, ::-1], c_(INITR),
                                         ALU.mult, ALU.add))
            phase_end(dve, "dve")

            def body(it):
                for s in range(2):
                    o = 0
                    for i, m in enumerate(PARTS):
                        dve.wait_ge(a0["mm"], it * 8 + s * 4 + i + 1)
                        V.tensor_copy(nd[:, bass.ds((it * 2 + s) * W + o, m * P)], ps_o[i % 2][:, 0:m * P]
                                      ).then_inc(a0["ev"], 1)
                        o += m * P
            rolled(dve, ITS, body)
            phase_end(dve, "dve")
            dve.wait_ge(lasts_in, 16 * LT)
            for t in range(1, LT):
                V.tensor_tensor(lasts[0], lasts[0], lasts[t], ALU.add).then_inc(lasts_sum, 1)
                dve.wait_ge(lasts_sum, t)
            dve.sem_inc(lasts_sum, 1)
            phase_end(dve, "dve")
            phase_end(dve, "dve")

            ch.link(V.memset(pay[:, :, :], 0.0))
            ch.link(V.memset(live[:, :], 0.0))
            ch.link(V.memset(sh[:, :, :], 0))
            ts(live[:, 0:J], rv[:, :], 0.5, None, ALU.is_gt)
            ts(t_e[:, 0:J], d_e[:, :], float(N), None, ALU.is_lt)
            tt(live[:, 0:J], live[:, 0:J], t_e[:, 0:J], ALU.mult)
            ch.link(V.tensor_tensor_scan(t_e[:, 0:J], ones[:, :], live[:, 0:J], 0.0, ALU.mult, ALU.add))
            cp(c_(CNT), t_e[:, J - 1:J])
            ts(t_f[:, 0:J], t_e[:, 0:J], part_c[:, 2:3], None, ALU.add)
            tt(t_f[:, 0:J], t_f[:, 0:J], live[:, 0:J], ALU.mult)
            cp(head[:, :], t_f[:, 0:J])
            tt(t_f[:, 0:J], col_i[:, 0:J], t_e[:, 0:J], ALU.subtract)
            tt(t_f[:, 0:J], t_f[:, 0:J], live[:, 0:J], ALU.mult)
            cp(sh[:, 0, 0:J], t_f[:, 0:J])
            cp(pay[:, 0, 0:J], rv[:, :])
            cp(pay[:, 1, 0:J], w_e[:, :])
            cp(pay[:, 2, 0:J], d_e[:, :])
            cp(pay[:, 3, 0:J], ddst[:, :])
            cp(pay[:, 4, 0:J], e_i[:, 0, :])
            cur = 0
            for b in range(9):
                k = 1 << b
                ts(mv[:, :], sh[:, cur, :], k, None, ALU.bitwise_and)
                ch.link(V.copy_predicated(pay[:, :, 0:JC - k], mv[:, k:JC].unsqueeze(1).to_broadcast([P, 5, JC - k]),
                                          pay[:, :, k:JC]))
                ch.link(V.scalar_tensor_tensor(sh[:, 1 - cur, :], mv[:, :], 0.0, sh[:, cur, :],
                                               ALU.is_equal, ALU.mult))
                ch.link(V.copy_predicated(sh[:, 1 - cur, 0:JC - k], mv[:, k:JC], sh[:, cur, k:JC]))
                cur = 1 - cur
            ts(live[:, :], col_i[:, :], c_(CNT), None, ALU.is_le)
            for i in (0, 1, 3, 4):
                tt(pay[:, i, :], pay[:, i, :], live[:, :], ALU.mult)
            ts(t_e[:, :], pay[:, 2, :], 1.0, None, ALU.add)
            tt(t_e[:, :], t_e[:, :], live[:, :], ALU.mult)
            red(c_(LC), t_e[:, :], ALU.max)
            ts(c_(LC), c_(LC), -1.0, None, ALU.add)
            ts(t_e[:, :], pay[:, 2, :], PADV, None, ALU.subtract)
            tt(t_e[:, :], t_e[:, :], live[:, :], ALU.mult)
            ts(pay[:, 2, :], t_e[:, :], PADV, None, ALU.add)
            cp(gidx[:, 0:JC], pay[:, 0, :])
            dc = pay[:, 2, :]
            cp(c_(FC), pay[:, 2, 0:1])
            tt(c_(POS), c_(CNT), part_c[:, 2:3], ALU.add)
            for i, m in enumerate((FC, LC, POS, CNT)):
                cp(lb[:, i * P:(i + 1) * P], c_(m).to_broadcast([P, P]))
            dve.sem_inc(cols_ready, 1)
            dve.wait_ge(spread, spread_no["r4"])
            ch.link(V.scalar_tensor_tensor(matc[:, :], ps_b[:, 0:P], c_(LC), before[:, :], ALU.is_equal, ALU.mult))
            red(c_(CONTC), matc[:, :])
            ts(c_(CONTC), c_(CONTC), 0.5, None, ALU.is_gt)
            ch.link(V.scalar_tensor_tensor(lb[:, 0:P], ps_b[:, P:2 * P], c_(FIRST), after[:, :],
                                           ALU.is_equal, ALU.mult))
            tt(lb[:, 0:P], lb[:, 0:P], ps_b[:, 2 * P:3 * P], ALU.mult)
            red(c_(CARP), lb[:, 0:P], ALU.max)
            ch.link(V.tensor_tensor_scan(t_e[:, 0:J], same[:, :], head[:, :], c_(CARP), ALU.mult, ALU.max))
            cp(ei[:, :, 0], t_e[:, 0:J])
            cp(ei[:, :, 1], deg[:, :])
            red(c_(T0), ps_b[:, 3 * P:4 * P], ALU.max)
            ts(c_(T0), c_(T0), float(2 * CB + 1), float(2 * CB - 1), ALU.max, ALU.add)
            cp(ci32[:, 2:3], c_(T0))
            ch.link(V.tensor_scalar(n_it[0:1, 0:1], ci32[0:1, 2:3], (2 * CB).bit_length() - 1, None,
                                    ALU.logical_shift_right))
            cp(sm[0:1, T0:T0 + 1], n_it[0:1, 0:1])
            ts(sm[0:1, T0:T0 + 1], sm[0:1, T0:T0 + 1], -1.0, None, ALU.add)
            cp(n_it[0:1, 1:2], sm[0:1, T0:T0 + 1])
            ch.link(V.memset(samec[:, 0:1], 1.0))
            tt(samec[:, 1:JC], pay[:, 2, 1:JC], pay[:, 2, 0:JC - 1], ALU.is_equal)
            ts(t_e[:, :], live[:, :], -1.0, 1.0, ALU.mult, ALU.add)
            tt(samec[:, :], samec[:, :], t_e[:, :], ALU.max)
            cp(maskc[:, 0:(JC // CB) * (CB + 1)].rearrange("p (b j) -> p b j", j=CB + 1)[:, :, 1:CB + 1],
               samec[:, :].rearrange("p (b j) -> p b j", j=CB))
            ch.link(V.memset(lastc[:, JC - 1:JC], 1.0))
            tt(lastc[:, 0:JC - 1], pay[:, 2, 0:JC - 1], pay[:, 2, 1:JC], ALU.not_equal)
            ts(t_e[:, :], dc, c_(LC), c_(CONTC), ALU.is_equal, ALU.mult)
            ts(t_e[:, :], t_e[:, :], -1.0, 1.0, ALU.mult, ALU.add)
            tt(lastc[:, :], lastc[:, :], t_e[:, :], ALU.mult)
            tt(lastc[:, :], lastc[:, :], live[:, :], ALU.mult)
            ts(t_e[:, :], dc, c_(FC), None, ALU.is_equal)
            tt(t_e[:, :], t_e[:, :], live[:, :], ALU.mult)
            red(c_(CFC), t_e[:, :])
            tt(head_c, t_e[:, :], lastc[:, :], ALU.mult)
            red(c_(HVC), head_c)
            tt(c_(T0), c_(FC), part_c[:, 0:1], ALU.subtract)
            tt(c_(T0), c_(T0), c_(HVC), ALU.mult)
            tt(c_(T0), c_(T0), part_c[:, 0:1], ALU.add)
            cp(ci32[:, 3:4], c_(T0))
            tt(c_(T0), c_(CFC), part_c[:, 2:3], ALU.add)
            tt(c_(T0), c_(T0), part_c[:, 1:2], ALU.subtract)
            tt(c_(T0), c_(T0), c_(HVC), ALU.mult)
            tt(c_(T0), c_(T0), part_c[:, 1:2], ALU.add)
            cp(ci32[:, 1:2], c_(T0))
            ts(t_e[:, :], dc, part_c[:, 0:1], None, ALU.subtract)
            tt(t_e[:, :], t_e[:, :], lastc[:, :], ALU.mult)
            ts(t_e[:, :], t_e[:, :], part_c[:, 0:1], None, ALU.add)
            cp(uidx[:, 0:JC], t_e[:, :])
            cp(srcc[:, 0:JC], pay[:, 4, :])
            rsqrt0(sdd[:, :], pay[:, 3, :], t_e[:, :], 1)
            tt(t_e[:, :], head_c, sdd[:, :], ALU.mult)
            red(sdh[:, 0:1], t_e[:, :])
            phase_end(dve, "dve")
            phase_end(dve, "dve")
            n = dve.value_load(n_it[0:1, 0:1], min_val=2, max_val=CN)
            phase_end(dve, "dve")
            cp(ridx[:, 0:JC], eg[:, 0:JC, 0])
            cp(t_f[:, :], eg[:, 0:JC, 1])
            rsqrt0(live[:, :], t_f[:, :], t_e[:, :], 2)
            tt(w1[:, 0:JC], pay[:, 1, :], live[:, :], ALU.mult)
            tt(w2[:, 0:JC], w1[:, 0:JC], live[:, :], ALU.mult)
            phase_end(dve, "dve")
            hop_chain.append(Chain(dve, "hop_chain"))
            fold_chain.append(Chain(dve, "fold_chain"))
            for c in range(2):
                for k in range(HOPS - 1):
                    hop_dve(dve, c * (HOPS - 1) + k, n)
                    phase_end(dve, "dve")
                fold_dve(dve, c, n)
                phase_end(dve, "dve")
                dense_dve(dve, c)
                phase_end(dve, "dve")

            lc = Chain(dve, "l_chain")
            V.memset(s_[1][:, :], 0.0).then_inc(l0, 1)
            dve.wait_ge(l0, 1)

            def body(it):
                lc.begin(it)
                for s in range(2):
                    dve.wait_ge(ls["gathered"][s], it * (16 * EB) + 16 * EB)
                    dve.wait_ge(ls["attr"][s], it * 16 + 16)
                    lc.link(V.tensor_tensor(fj(v_[s], EB + 1)[:, :, 1:EB + 1], jf(g_[s], EB), jf(a_[s], EB), ALU.mult))
                    if not (first(it) and s == 0):
                        dve.wait_ge(ls["scanned"], it * 2 + s)
                    lc.link(V.tensor_copy(fj(v_[s], EB + 1)[:, :, 0:1], fj(s_[1 - s], EB + 1)[:, :, EB:EB + 1]))
                    dve.wait_ge(ls["masked"][s], it + 1)
                    V.tensor_tensor_scan(s_[s], m_[s], v_[s], 0.0, ALU.mult, ALU.add).then_inc(ls["scanned"], 1)
                    dve.wait_ge(ls["scanned"], it * 2 + s + 1)
                    if not first(it):
                        for t in range(ST):
                            dve.wait_ge(ls["scattered"][t], (it * 2 + s - 1) * (16 * EB // ST))
                    V.tensor_tensor(jf(r_[s], EB), fj(s_[s], EB + 1)[:, :, 1:EB + 1],
                                    over_f(rcnt[:, bass.ds((it * 2 + s) * EB, EB)]), ALU.mult
                                    ).then_inc(ls["ready"][s], 1)
                lc.end()
            rolled(dve, ITS, body)
            dve.wait_ge(spread, spread_no["l1"])
            V.tensor_scalar(carry[:, :], ps_c[:, 0:D], c_(RCH), None, ALU.mult).then_inc(ls["carried"], 1)
            phase_end(dve, "dve")
            dense_dve(dve, 2)
            phase_end(dve, "dve")


_INS = ["x", "src", "dst", "edge_attr_32", "edge_weight", "node_vec",
        "node_vec_n2", "node_vec_n3",
        "L0_gnn_W0", "L0_gnn_b0", "L0_gnn_W1", "L0_gnn_b1"]


def kernel(**inputs):
    import numpy as np
    import concourse.bacc as bacc
    from concourse.bass_utils import run_bass_kernel_spmd

    nc = bacc.Bacc("TRN2", target_bir_lowering=False, num_devices=1)
    arrays, args = {}, []
    for name in _INS:
        a = np.ascontiguousarray(inputs[name])
        arrays[f"in_{name}"] = a
        args.append(nc.dram_tensor(f"in_{name}", a.shape, mybir.dt.from_np(a.dtype), kind="ExternalInput").ap())
    args.append(nc.dram_tensor("out_rows", (N, D), F32, kind="ExternalOutput").ap())
    gnn_program(nc, *args)
    r = run_bass_kernel_spmd(nc, [arrays], core_ids=[0])
    return r.results[0]["out_rows"]
```

```python
import concourse.bass as bass
from concourse import mybir
from contextlib import ExitStack

F32 = mybir.dt.float32
I32 = mybir.dt.int32
ALU = mybir.AluOpType
ACT = mybir.ActivationFunctionType
AX = mybir.AxisListType

P = 128
N = 100000
E = 50000
D = 32
HOPS = 3
EPS = 1e-5
SLOPE = 0.01

J = 392
EP = P * J
EB = 28
JC = 400
CB = 8
CN = JC // (2 * CB)
JX = JC + 2 * CB
NB = 56
NBLK = 14
NP = P * NB * NBLK
LASTP, LASTC = (N - (NBLK - 1) * P * NB) // NB, (N - (NBLK - 1) * P * NB) % NB
ITS = 7
PADV = 200000.0
TROWS = P * JC
LT = 7
ST = 2
PER = 16 * CB // ST
LEAD = 6
HT = 20
GC = 4


def gnn_program(nc, x, src, dst, attr, weight, nv, gamma, beta, W0, b0, W1, b1, out):
    ctx = ExitStack()
    with ctx:
        def sb(name, shape, dt=F32):
            return ctx.enter_context(nc.sbuf_tensor(name, shape, dt))

        def sem(name):
            return ctx.enter_context(nc.semaphore(name))

        def sems(name):
            return [sem(f"{name}{s}") for s in range(2)]

        def dram(name, shape, dt=F32):
            return nc.dram_tensor(name, shape, dt, kind="Internal").ap()

        e_src = dram("e_src", (EP,), I32)
        e_dst = dram("e_dst", (EP + 1,), I32)
        e_w = dram("e_w", (EP,))
        e_attr = dram("e_attr", (EP, D))
        u_attr = dram("u_attr", (EP, D))
        node_lasts = [dram(f"node_lasts{k}", (NP + P, 1)) for k in range(LT)]
        node_last = dram("node_last", (NP + P, 1))
        edge_info = dram("edge_info", (1 + EP, 2))
        node_sum = [dram(f"node_sum{k}", (NP + P, D)) for k in range(ST)]
        agg_sum = [dram(f"agg_sum{k}", (NP + P, D)) for k in range(ST)]
        x_cent = dram("x_cent", (NP, D))
        node_tab = dram("node_tab", (NP, D))
        hop_tab = [dram(f"hop_tab{k}", (1 + TROWS + P, D)) for k in range(HOPS - 1)]

        ident = sb("ident", [P, P])
        cmat = sb("cmat", [P, P])
        before = sb("before", [P, P])
        after = sb("after", [P, P])
        ones = sb("ones", [P, J])
        zeros = sb("zeros", [P, (NP + P) // P])
        col_i = sb("col_i", [P, JC])
        part_c = sb("part_c", [P, 4])
        padi = sb("padi", [1, EP + 1 - E], I32)
        bd = sb("bd", [P, 2 * (HOPS + 1) * P])
        brow = sb("brow", [1, 2 * 512])

        e_i = sb("e_i", [P, 2, J], I32)
        same = sb("same", [P, J])
        rcnt = sb("rcnt", [P, J])
        sidx = sb("sidx", [P, J], I32)
        mat = sb("mat", [P, P])
        sm = sb("sm", [P, 48])
        ci32 = sb("ci32", [P, 4], I32)
        w1 = sb("w1", [P, JX])
        w2 = sb("w2", [P, JX])
        gidx = sb("gidx", [P, JX], I32)
        srcc = sb("srcc", [P, JX], I32)
        ridx = sb("ridx", [P, JX], I32)
        uidx = sb("uidx", [P, JX], I32)
        sdd = sb("sdd", [P, JC])
        lastc = sb("lastc", [P, JC])
        samec = sb("samec", [P, JC])
        maskc = sb("maskc", [P, JX // CB * (CB + 1)])
        maske = sb("maske", [P, (J // EB + 2) * (EB + 1)])
        sdh = sb("sdh", [P, 1])
        matc = sb("matc", [P, P])
        n_it = sb("n_it", [1, 2], I32)

        nd = sb("nd", [P, NBLK * NB * D])
        nvs = sb("nvs", [P, NBLK * NB])
        carry = sb("carry", [P, D])
        istage = [sb(f"istage{s}", [P, EB], I32) for s in range(2)]
        eidx_ = [sb(f"eidx{s}", [P, EB], I32) for s in range(2)]
        work = sb("work", [P, 2 * 4 * NB * D])
        W = NB * D

        def slotv(s, off, n):
            return work[:, s * 4 * W + off:s * 4 * W + off + n]

        g_ = [slotv(s, 0, EB * D) for s in range(2)]
        v_ = [slotv(s, 896, (EB + 1) * D) for s in range(2)]
        s_ = [slotv(s, 1824, (EB + 1) * D) for s in range(2)]
        m_ = [slotv(s, 2752, (EB + 1) * D) for s in range(2)]
        r_ = [slotv(s, 3680, EB * D) for s in range(2)]
        a_ = [slotv(s, 4576, EB * D) for s in range(2)]
        tl_ = [slotv(s, 4576, (HOPS - 1) * CB * D) for s in range(2)]
        hb_ = [slotv(s, 5088, CB * D) for s in range(2)]
        tt_ = [slotv(s, 5344, HOPS * P) for s in range(2)]
        zb_ = [slotv(s, 4576, W // 2) for s in range(2)]
        xc_ = [slotv(s, 5472, W // 2) for s in range(2)]
        ub = [slotv(s, 0, W) for s in range(2)]
        cb = [slotv(s, W, W) for s in range(2)]
        xb = [slotv(s, 3 * W, W) for s in range(2)]
        at = [0, 4 * W]

        def early(s, *shape, dt=F32):
            n = 1
            for d in shape:
                n *= d
            t = work[:, at[s]:at[s] + n]
            at[s] += n
            assert at[s] <= s * 4 * W + 3 * W
            if dt != F32:
                t = t.bitcast(dt)
            if len(shape) == 2:
                t = t.rearrange("p (a b) -> p a b", a=shape[0])
            return t

        pay = early(0, 5, JC)
        sh = early(0, 2, JC, dt=I32)
        mv = early(0, JC, dt=I32)
        t_e = early(0, JC)
        t_f = early(0, JC)
        lb = early(0, 4 * P)
        live = early(0, JC)
        d_e = early(1, J)
        w_e = early(1, J)
        edge_no = early(1, J)
        last = early(1, J)
        head = early(1, J)
        deg = early(1, J)
        cnt = early(1, J)
        ddst = early(1, J)
        rv = early(1, J)
        eg = early(1, JX, 2)
        ei = early(1, J, 2)
        mat2 = early(1, P)

        OB = 14
        pairs = nd[:, 0:OB * J].rearrange("p (a b) -> p a b", b=J)
        pairs2 = nd[:, OB * J:2 * OB * J].rearrange("p (a b) -> p a b", b=J)
        o_at = 2 * OB * J
        rank, less, d_tie, row_f = [nd[:, o_at + i * J:o_at + (i + 1) * J] for i in range(4)]
        row_i = nd[:, o_at + 4 * J:o_at + 5 * J].bitcast(I32)
        rank_i = nd[:, o_at + 5 * J:o_at + 6 * J].bitcast(I32)
        o_attr = nd[:, o_at + 6 * J:o_at + 6 * J + EB * D]
        d_next = rv.bitcast(I32)

        lasts = [work[:, t * (NP + P) // P:(t + 1) * (NP + P) // P] for t in range(LT)]

        xt = [sb(f"xt{i}", [P, 4 * P]) for i in range(2)]
        gb = [sb(f"gb{s}", [P, 2 * NB]) for s in range(2)]
        st = [sb(f"st{s}", [P, 2 * NB]) for s in range(2)]

        ps_t = [ctx.enter_context(nc.psum_tensor(f"ps_t{i}", [P, 512], F32)) for i in range(2)]
        ps_o = [ctx.enter_context(nc.psum_tensor(f"ps_o{i}", [P, 512], F32)) for i in range(2)]
        ps_x = [ctx.enter_context(nc.psum_tensor(f"ps_x{i}", [P, 512], F32)) for i in range(2)]
        ps_b = ctx.enter_context(nc.psum_tensor("ps_b", [P, 512], F32))
        ps_c = ctx.enter_context(nc.psum_tensor("ps_c", [P, 512], F32))

        def b_split(t, r):
            return t.rearrange("(a b) -> a b", a=r)

        def ev(t):
            return t.rearrange("(p j) -> p j", p=P)

        attr_v = e_attr.rearrange("(p j) f -> p (j f)", p=P)

        def hop_rows(k):
            return hop_tab[k][1:1 + TROWS, :].rearrange("(p j) f -> p (j f)", p=P)

        def node_rows(t, b):
            return t[bass.ds(b * (P * NB), P * NB), :].rearrange("(p c) f -> p (c f)", p=P)

        def fj(t, n):
            return t[:, 0:D * n].rearrange("p (f j) -> p f j", f=D)

        def jf(t, n):
            return t[:, 0:D * n].rearrange("p (j f) -> p f j", f=D)

        def over_f(t):
            return t.unsqueeze(1).to_broadcast([P, D, t.shape[1]])

        def over_row(t):
            return t.unsqueeze(2).to_broadcast([P, t.shape[1], D])

        def rows(t, n=NB):
            return t.rearrange("p (c f) -> p c f", f=D)

        def zero_block(eng, t, it, s):
            h = W // 4
            eng.dma_start(node_rows(t, it * 2 + s).rearrange("p (a b) -> p a b", a=4),
                          zeros[:, 0:h].unsqueeze(1).to_broadcast([P, 4, h])).then_inc(big0, 16)

        phase_done = sem("phase_done")
        phase_no = {}

        def phase_end(eng, name):
            phase_no[name] = phase_no.get(name, 0) + 1
            eng.drain().then_inc(phase_done, 1)
            eng.wait_ge(phase_done, 5 * phase_no[name])

        def so_far(round, turns, it, per, more, extra=0):
            at = it * per + more + round * extra
            return at if round == 0 else turns * (round * per) + at

        class Chain:

            def __init__(self, eng, name):
                self.eng, self.sem, self.n, self.per, self.it = eng, sem(name), 0, 0, 0
                self.round, self.turns = 0, 0

            def begin(self, it, round=0, turns=0):
                self.it, self.n, self.round, self.turns = it, 0, round, turns

            def link(self, ins):
                self.n += 1
                ins.then_inc(self.sem, 1)
                self.eng.wait_ge(self.sem, so_far(self.round, self.turns, self.it, self.per, self.n))

            def end(self):
                self.per = self.n

        def rolled(eng, count, body, upto=None, last_apart=0):
            body(0)
            with eng.Fori(1, count - last_apart) as it:
                if upto is None:
                    body(it)
                else:
                    with eng.If(it < upto):
                        body(it)
            for it in range(count - last_apart, count):
                body(it)

        def rolled_beside(eng, upto, parts, sides, side_turns):
            def both(it):
                for part, side in zip(parts, sides):
                    part(it)
                    side(it)
            both(0)
            with eng.Fori(1, side_turns) as it:
                both(it)
            with eng.Fori(side_turns, CN) as it:
                with eng.If(it < upto):
                    for part in parts:
                        part(it)

        def first(it):
            return isinstance(it, int) and it == 0

        copied = sem("copied")
        order_seen = sem("order_seen")
        row_in = sem("row_in")
        row_used = sem("row_used")
        o_loaded = sem("o_loaded")
        o_staged = sem("o_staged")
        o_moved = sem("o_moved")
        o_block = sem("o_block")
        attr_in = sem("attr_in")
        reloaded = sem("reloaded")
        zeroed = sem("zeroed")
        tabs0 = sem("tabs0")
        big0 = sem("big0")
        consts = sem("consts")
        loaded = sem("loaded")
        cols_ready = sem("cols_ready")
        spread = sem("spread")
        info_out = sem("info_out")
        wts = sem("wts")
        wts_done = sem("wts_done")
        consts_ready = sem("consts_ready")
        bd0 = sem("bd0")
        act_own = sem("act_own")
        root_in = sem("root_in")
        root_out = sem("root_out")
        lasts_in = sem("lasts_in")
        lasts_sum = sem("lasts_sum")
        gb_in = sems("gb_in")
        l0 = sem("l0")

        def hop_sems(tag):
            return dict(gathered=sems(f"gat_{tag}"), staged=sems(f"stg_{tag}"), masked=sems(f"msk_{tag}"),
                        scanned=sem(f"scn_{tag}"), rowed=sem(f"row_{tag}"), written=sems(f"wrt_{tag}"),
                        carried=sem(f"car_{tag}"))

        hs = hop_sems("hop")
        hop_chain = []
        fs = dict(gathered=sems("fga"), staged=sems("fst"), masked=sems("fmk"), scanned=sem("fsc"), rowed=sem("frw"),
                  carried=sem("fca"), loaded=sems("fld"), transposed=sem("ftr"), copied=sem("fcp"), mult=sem("fmm"),
                  ready=sems("frd"), scattered=[sem(f"fsx{t}") for t in range(ST)])
        fold_chain = []
        rs = dict(staged=sems("rstg"), scattered=[sem(f"rsct{t}") for t in range(LT)])
        rg = dict(staged=sems("gstg"), gathered=sems("ggat"))
        eg_s = dict(staged=sems("estg"), gathered=sems("egat"))
        a0 = dict(xl=sems("a0x"), xst=sems("a0s"), tr=sem("a0t"), cp=sem("a0c"), mm=sem("a0m"), ev=sem("a0e"))
        dense = [dict(ul=sems(f"dul{i}_"), cen=sem(f"dce{i}"), sq=sem(f"dsq{i}"), var=sem(f"dva{i}"),
                      both=sem(f"dbo{i}"), root=sem(f"dro{i}"), done=sem(f"ddn{i}"), stored=sems(f"dst{i}_"),
                      chain=f"dch{i}") for i in range(3)]
        dense[0].update(scaled=sem("dsc0"), shifted=sem("dsh0"))
        bs = dict(rows=sems("brw"), tr=sem("btr"), cp=sem("bcp"), mm=sem("bmm"), ev=sem("bev"), withx=sem("bwx"))
        centred = sem("centred")
        ls = dict(attr=sems("lat"), gathered=sems("lga"), staged=sems("lst"), masked=sems("lmk"), scanned=sem("lsc"),
                  ready=sems("lrd"), scattered=sems("lsx"), carried=sem("lca"))

        block = ctx.enter_context(nc.Block())

        def attr_copy(sp, to):
            sp.dma_start(to[0:E, :].rearrange("(a b) f -> a (b f)", a=16),
                         attr.rearrange("(a b) f -> a (b f)", a=16)).then_inc(attr_in, 16)
            sp.dma_start(to[E:EP, :].rearrange("(p a) f -> p (a f)", a=2), zeros[0:(EP - E) // 2, 0:2 * D]
                         ).then_inc(attr_in, 16)
            sp.wait_ge(attr_in, 32)

        def order_sp(sp):
            attr_copy(sp, u_attr)
            def body(r):
                if not first(r):
                    sp.wait_ge(row_used, r)
                    sp.sem_inc(sp_step, 1)
                sp.dma_start(row_i, e_dst[bass.ds(r * J, J)].rearrange("(a b) -> a b", a=1).to_broadcast([P, J])
                             ).then_inc(row_in, 16)
            rolled(sp, P, body)

            def body(b):
                if not first(b):
                    sp.wait_ge(o_block, b)
                    sp.sem_inc(sp_step, 1)
                sp.dma_start(o_attr, u_attr.rearrange("(p j) f -> p (j f)", p=P)[:, bass.ds(b * (EB * D), EB * D)]
                             ).then_inc(o_loaded, 16)
            rolled(sp, NBLK, body)
            sp.wait_ge(o_block, NBLK)
            sp.dma_start(e_i[:, 0, :], ev(e_src)).then_inc(reloaded, 16)
            sp.dma_start(e_i[:, 1, :], ev(e_dst[0:EP])).then_inc(reloaded, 16)
            sp.dma_start(w_e[:, :], ev(e_w)).then_inc(reloaded, 16)

        def order_dve(dve):
            V = nc.vector
            V.tensor_copy(sm[:, 24:25], part_c[:, 3:4])
            V.memset(rank, 0.0)
            dve.drain()

            def compare(to, a, b, op, b_cols):
                V.tensor_tensor(to, a.unsqueeze(1).to_broadcast([P, OB, J]),
                                b[:, b_cols * OB:(b_cols + 1) * OB].unsqueeze(2).to_broadcast([P, OB, J]), op)

            def body(r):
                dve.wait_ge(row_in, r * 16 + 16)
                V.tensor_copy(row_f, row_i)
                V.tensor_scalar(sm[:, 25:26], sm[:, 24:25], 0.5, 0.5, ALU.is_gt, ALU.mult)
                dve.drain()
                V.tensor_scalar(d_tie, d_e[:, :], sm[:, 25:26], None, ALU.add)
                V.tensor_scalar(sm[:, 24:25], sm[:, 24:25], float(-J), None, ALU.add)
                dve.drain()
                for b in range(J // OB):
                    compare(pairs, row_f, d_tie, ALU.is_lt, b)
                    dve.drain()
                    V.tensor_reduce(less[:, b * OB:(b + 1) * OB], pairs, AX.X, ALU.add)
                    dve.drain()
                V.tensor_tensor(rank, rank, less, ALU.add)
                dve.drain().then_inc(row_used, 1)
            rolled(dve, P, body)
            for b in range(J // OB):
                compare(pairs, d_e[:, :], d_e, ALU.is_equal, b)
                compare(pairs2, col_i[:, 0:J], col_i, ALU.is_lt, b)
                dve.drain()
                V.tensor_tensor(pairs, pairs, pairs2, ALU.mult)
                dve.drain()
                V.tensor_reduce(less[:, b * OB:(b + 1) * OB], pairs, AX.X, ALU.add)
                dve.drain()
            V.tensor_tensor(rank, rank, less, ALU.add)
            dve.drain()
            V.tensor_copy(rank_i, rank)
            dve.drain()

            def body(b):
                if not first(b):
                    dve.wait_ge(o_block, b)
                cols = bass.ds(b * EB, EB)
                V.tensor_copy(istage[0][:, :], rank_i[:, cols])
                V.tensor_copy(istage[1][:, :], e_i[:, 0, cols])
                V.tensor_copy(eidx_[0][:, :], e_i[:, 1, cols])
                V.tensor_copy(st[0][:, 0:EB], w_e[:, cols])
                dve.drain().then_inc(o_staged, 1)
            rolled(dve, NBLK, body)
            dve.wait_ge(reloaded, 48)
            V.tensor_copy(d_e[:, :], e_i[:, 1, :])
            dve.drain()

        def order_pool(pool):
            def body(b):
                pool.wait_ge(o_staged, b + 1)
                pool.wait_ge(o_loaded, b * 16 + 16)
                pool.sem_inc(pool_step, 1)
                for j in range(EB):
                    for to, data in ((e_src, istage[1][:, j:j + 1]), (e_dst[0:EP], eidx_[0][:, j:j + 1]),
                                     (e_w, st[0][:, j:j + 1]), (e_attr, o_attr[:, j * D:(j + 1) * D])):
                        pool.indirect_dma_start(
                            out=to if data.shape[1] == D else to.rearrange("(a b) -> a b", b=1),
                            out_offset=bass.IndirectOffsetOnAxis(ap=istage[0][:, j:j + 1], axis=0),
                            in_=data, in_offset=None).then_inc(o_moved, 16)
                    pool.wait_ge(o_moved, b * (64 * EB) + 64 * (j + 1))
                    pool.sem_inc(pool_step, 1)
                pool.sem_inc(o_block, 1)
            rolled(pool, NBLK, body)

        HALF = [4, 3]

        def side_sp(sp, k, it, s):
            b = it + ITS * k
            for t, to in ((node_tab, zb_), (x_cent, xc_)):
                sp.dma_start(to[s], node_rows(t, b)[:, s * (W // 2):(s + 1) * (W // 2)]).then_inc(bs["rows"][s], 16)

        def side_pe(pe, k, it):
            b = it + ITS * k
            for s in range(2):
                pe.wait_ge(bs["rows"][s], b * 32 + 32)
                at = 0
                fresh = first(b) and s == 0
                for i, m in enumerate(HALF):
                    no = b * 4 + s * 2 + i
                    if not fresh:
                        pe.wait_ge(bs["cp"], no - 1)
                    for g in range(m):
                        ins = nc.tensor.transpose(ps_t[i][:, g * P:(g + 1) * P],
                                                  zb_[s][:, at + g * P:at + (g + 1) * P], ident[:, :])
                    ins.then_inc(bs["tr"], 1)
                    at += m * P
                for i, m in enumerate(HALF):
                    no = b * 4 + s * 2 + i
                    pe.wait_ge(bs["cp"], no + 1)
                    if not fresh:
                        pe.wait_ge(bs["ev"], no - 1)
                    for g in range(m):
                        to = ps_o[i][:, g * P:(g + 1) * P]
                        nc.tensor.matmul(to, xt[i][:, g * P:(g + 1) * P],
                                         bd[:, (HOPS + 1) * P:(HOPS + 2) * P], start=True, stop=False)
                        ins = nc.tensor.matmul(to, ones[0:1, 0:P], brow[0:1, 512:512 + P], start=False, stop=True)
                    ins.then_inc(bs["mm"], 1)

        def side_act(act, k, it, s):
            b = it + ITS * k
            for i, m in enumerate(HALF):
                no = b * 4 + s * 2 + i
                act.wait_ge(bs["tr"], no + 1)
                if not (first(b) and s == 0):
                    act.wait_ge(bs["mm"], no - 1)
                nc.scalar.copy(xt[i][:, 0:m * P], ps_t[i][:, 0:m * P]).then_inc(bs["cp"], 1)

        def side_dve(dve, k, it, s):
            b = it + ITS * k
            o = s * (W // 2)
            half = nd[:, bass.ds(b * W + o, W // 2)]
            for i, m in enumerate(HALF):
                dve.wait_ge(bs["mm"], b * 4 + s * 2 + i + 1)
                nc.vector.tensor_tensor(rows(nd[:, bass.ds(b * W + o, m * P)]), rows(ps_o[i][:, 0:m * P]),
                                        over_row(nvs[:, bass.ds(b * NB + o // D, m * GC)]), ALU.mult
                                        ).then_inc(bs["ev"], 1)
                o += m * P
            dve.wait_ge(bs["ev"], b * 4 + s * 2 + 2)
            dve.wait_ge(bs["rows"][s], b * 32 + 32)
            nc.vector.tensor_tensor(half, half, xc_[s], ALU.add).then_inc(bs["withx"], 1)

        def hop_sp(sp, h, n):
            q, k = hs, h % (HOPS - 1)

            def part(s):
                def body(it):
                    sp.wait_ge(q["rowed"], so_far(h, n, it, 2, s + 1))
                    sp.dma_start(hop_rows(k)[:, bass.ds(it * (2 * CB * D) + s * CB * D, CB * D)],
                                 r_[s][:, 0:CB * D]).then_inc(q["written"][s], 16)
                return body
            if h < HOPS - 1:
                rolled(sp, CN, lambda it: [part(s)(it) for s in range(2)], n)
                return

            def side(s):
                def body(it):
                    sp.wait_ge(bs["withx"], (it + ITS * k) * 2 + s + 1)
                    sp.sem_inc(sp_step, 1)
                    side_sp(sp, k, it + 1, s)
                return body
            for s in range(2):
                side_sp(sp, k, 0, s)
            rolled_beside(sp, n, [part(0), part(1)], [side(0), side(1)], ITS - 1)

        def hop_act(act, h, n):
            q, k = hs, h % (HOPS - 1)
            idx = srcc if k == 0 else ridx

            def stage(it, s):
                col = it * (2 * CB) + s * CB
                nc.scalar.copy(istage[s][:, 0:CB], idx[:, bass.ds(col, CB)]).then_inc(q["staged"][s], 1)
                nc.scalar.copy(fj(m_[s], CB + 1),
                               over_f(maskc[:, bass.ds(it * (2 * (CB + 1)) + s * (CB + 1), CB + 1)])
                               ).then_inc(q["masked"][s], 1)

            def part(s):
                def body(it):
                    act.wait_ge(q["scanned"], so_far(h, n, it, 2, s + 1))
                    if not first(it):
                        act.wait_ge(q["written"][s], so_far(h, n, it, 16, 0))
                    nc.scalar.copy(jf(r_[s], CB), fj(s_[s], CB + 1)[:, :, 1:CB + 1]).then_inc(q["rowed"], 1)
                    stage(it + 1, s)
                return body

            def side(s):
                return lambda it: side_act(act, k, it, s)
            for s in range(2):
                stage(0, s)
            if h < HOPS - 1:
                rolled(act, CN, lambda it: [part(s)(it) for s in range(2)], n)
            else:
                rolled_beside(act, n, [part(0), part(1)], [side(0), side(1)], ITS)

        def hop_dve(dve, h, n):
            q, k = hs, h % (HOPS - 1)
            wt = w1 if k == 0 else w2
            ch = hop_chain[0]
            nc.vector.memset(s_[1][:, 0:D * (CB + 1)], 0.0).then_inc(q["carried"], 1)
            dve.wait_ge(q["carried"], 2 * h + 1)

            def part(s):
                def body(it):
                    if s == 0:
                        ch.begin(it, h, n)
                    dve.wait_ge(q["gathered"][s], so_far(h, n, it, 16 * CB, 16 * CB))
                    ch.link(nc.vector.tensor_tensor(fj(v_[s], CB + 1)[:, :, 1:CB + 1], jf(g_[s], CB),
                                                    over_f(wt[:, bass.ds(it * (2 * CB) + s * CB, CB)]), ALU.mult))
                    if not (first(it) and s == 0):
                        dve.wait_ge(q["scanned"], so_far(h, n, it, 2, s))
                    ch.link(nc.vector.tensor_copy(fj(v_[s], CB + 1)[:, :, 0:1], fj(s_[1 - s], CB + 1)[:, :, CB:CB + 1]))
                    dve.wait_ge(q["masked"][s], so_far(h, n, it, 1, 1, 1))
                    nc.vector.tensor_tensor_scan(s_[s][:, 0:D * (CB + 1)], m_[s][:, 0:D * (CB + 1)],
                                                 v_[s][:, 0:D * (CB + 1)], 0.0, ALU.mult, ALU.add
                                                 ).then_inc(q["scanned"], 1)
                    if s == 1:
                        ch.end()
                return body

            def side(s):
                return lambda it: side_dve(dve, k, it, s)
            if h < HOPS - 1:
                rolled(dve, CN, lambda it: [part(s)(it) for s in range(2)], n)
            else:
                rolled_beside(dve, n, [part(0), part(1)], [side(0), side(1)], ITS)
            dve.wait_ge(spread, spread_no[f"h{h}"])
            nc.vector.tensor_copy(carry[:, :], ps_c[:, 0:D]).then_inc(q["carried"], 1)

        def hop_pe(pe, h, n):
            q = hs
            if h >= HOPS - 1:
                rolled(pe, ITS, lambda it: side_pe(pe, h % (HOPS - 1), it))
            pe.wait_ge(q["scanned"], n * (2 * (h + 1)))
            nc.tensor.matmul(ps_c[:, 0:D], matc[:, :], fj(s_[1], CB + 1)[:, :, CB], start=True, stop=True
                             ).then_inc(spread, 1)

        def scatter(pool, tabs, idx, data, done, it, s, j, per, round=0, turns=0):
            k = len(tabs)
            before_it = (s * per + j) // k
            if not (first(it) and before_it == 0):
                pool.wait_ge(done[j % k], so_far(round, turns, it, 2 * 16 * per // k, 16 * before_it))
                pool.sem_inc(pool_step, 1)
            pool.indirect_dma_start(out=tabs[j % k], out_offset=bass.IndirectOffsetOnAxis(ap=idx, axis=0),
                                    in_=data, in_offset=None).then_inc(done[j % k], 16)

        def hop_pool(pool, h, n):
            q, k = hs, h % (HOPS - 1)
            tab = (x if h == 0 else node_tab) if k == 0 else hop_tab[k - 1]

            def body(it):
                for s in range(2):
                    pool.wait_ge(q["staged"][s], so_far(h, n, it, 1, 1, 1))
                    pool.sem_inc(pool_step, 1)
                    for j in range(CB):
                        pool.indirect_dma_start(
                            out=g_[s][:, j * D:(j + 1) * D], out_offset=None, in_=tab,
                            in_offset=bass.IndirectOffsetOnAxis(ap=istage[s][:, j:j + 1], axis=0)
                        ).then_inc(q["gathered"][s], 16)
            rolled(pool, CN, body, n)
            for s in range(2):
                pool.wait_ge(q["written"][s], n * (16 * (h + 1)))
            pool.wait_ge(q["carried"], 2 * h + 2)
            pool.sem_inc(pool_step, 1)
            pool.indirect_dma_start(out=hop_tab[k], out_offset=bass.IndirectOffsetOnAxis(ap=ci32[:, 1:2], axis=0),
                                    in_=carry[:, :], in_offset=None, compute_op=ALU.add).then_inc(fixed, 16)
            nfix[0] += 1
            pool.wait_ge(fixed, 16 * nfix[0])

        fixed = sem("fixed")
        nfix = [0]
        pool_step = sem("pool_step")
        sp_step = sem("sp_step")
        spread_no = {"r1": 1, "r2": 2, "r3": 3, "r4": 4}
        for c in range(2):
            for k in range(HOPS - 1):
                spread_no[f"h{c * (HOPS - 1) + k}"] = 5 + c * (HOPS + 1) + k
            spread_no[f"f{c}"] = 5 + c * (HOPS + 1) + HOPS - 1
        spread_no["l1"] = 5 + 2 * (HOPS + 1)

        def fold_sp(sp, c, n):
            q = fs

            def body(it):
                for s in range(2):
                    if not first(it):
                        sp.wait_ge(q["transposed"], so_far(c, n, it, 4, s * 2 - 2))
                    for k in range(HOPS - 1):
                        sp.dma_start(tl_[s][:, k * CB * D:(k + 1) * CB * D],
                                     hop_rows(k)[:, bass.ds(it * (2 * CB * D) + s * CB * D, CB * D)]
                                     ).then_inc(q["loaded"][s], 16)
            rolled(sp, CN, body, n)

        def fold_act(act, c, n):
            q = fs

            def stage(it, s):
                nc.scalar.copy(istage[s][:, 0:CB], ridx[:, bass.ds(it * (2 * CB) + s * CB, CB)]
                               ).then_inc(q["staged"][s], 1)
                nc.scalar.copy(fj(m_[s], CB + 1),
                               over_f(maskc[:, bass.ds(it * (2 * (CB + 1)) + s * (CB + 1), CB + 1)])
                               ).then_inc(q["masked"][s], 1)

            def body(it):
                for s in range(2):
                    act.wait_ge(q["scanned"], so_far(c, n, it, 2, s + 1))
                    stage(it + 1, s)
                    if not first(it):
                        act.wait_ge(q["transposed"], so_far(c, n, it, 4, s * 2 - 2))
                        for t in range(ST):
                            act.wait_ge(q["scattered"][t], so_far(c, n, it, 2 * PER, (s - 1) * PER))
                    nc.scalar.copy(jf(hb_[s], CB), fj(s_[s], CB + 1)[:, :, 1:CB + 1]).then_inc(q["rowed"], 1)
                    nc.scalar.copy(eidx_[s][:, 0:CB], uidx[:, bass.ds(it * (2 * CB) + s * CB, CB)]
                                   ).then_inc(q["ready"][s], 1)
                    for g in range(2):
                        act.wait_ge(q["transposed"], so_far(c, n, it, 4, s * 2 + g + 1))
                        if not (first(it) and s == 0):
                            act.wait_ge(q["mult"], so_far(c, n, it, 4, s * 2 + g - 1))
                        nc.scalar.copy(tt_[g][:, :], ps_t[g][:, 0:HOPS * P]).then_inc(q["copied"], 1)
            for s in range(2):
                stage(0, s)
            rolled(act, CN, body, n)

        def fold_pe(pe, c, n):
            q = fs

            def body(it):
                for s in range(2):
                    pe.wait_ge(q["loaded"][s], so_far(c, n, it, 16 * (HOPS - 1), 16 * (HOPS - 1)))
                    pe.wait_ge(q["rowed"], so_far(c, n, it, 2, s + 1))
                    for g in range(2):
                        if not (first(it) and s == 0):
                            pe.wait_ge(q["copied"], so_far(c, n, it, 4, s * 2 + g - 1))
                        for k in range(HOPS):
                            of = hb_[s][:, g * P:(g + 1) * P] if k == HOPS - 1 else \
                                tl_[s][:, (2 * k + g) * P:(2 * k + g + 1) * P]
                            ins = nc.tensor.transpose(ps_t[g][:, k * P:(k + 1) * P], of, ident[:, :])
                        ins.then_inc(q["transposed"], 1)
                    if not first(it):
                        pe.wait_ge(q["ready"][s], so_far(c, n, it, 2, 0))
                    for g in range(2):
                        pe.wait_ge(q["copied"], so_far(c, n, it, 4, s * 2 + g + 1))
                        for k in range(HOPS):
                            ins = nc.tensor.matmul(ps_o[s][:, g * P:(g + 1) * P], tt_[g][:, k * P:(k + 1) * P],
                                                   bd[:, (c * (HOPS + 1) + k + 1) * P:(c * (HOPS + 1) + k + 2) * P],
                                                   start=(k == 0), stop=(k == HOPS - 1))
                        ins.then_inc(q["mult"], 1)
            rolled(pe, CN, body, n)
            pe.wait_ge(q["scanned"], n * (2 * (c + 1)))
            nc.tensor.matmul(ps_c[0:D, 0:P], fj(s_[1], CB + 1)[:, :, CB], matc[:, :], start=True, stop=True
                             ).then_inc(spread, 1)
            pe.wait_ge(q["carried"], 3 * c + 2)
            w0 = (c * (HOPS + 1) + HOPS) * P
            nc.tensor.matmul(ps_b[:, 0:D], tt_[0][0:D, 0:P], bd[0:D, w0:w0 + D], start=True, stop=True
                             ).then_inc(spread, 1)

        def fold_dve(dve, c, n):
            q = fs
            ch = fold_chain[0]
            nc.vector.memset(s_[1][:, 0:D * (CB + 1)], 0.0).then_inc(q["carried"], 1)
            dve.wait_ge(q["carried"], 3 * c + 1)

            def body(it):
                ch.begin(it, c, n)
                for s in range(2):
                    dve.wait_ge(q["gathered"][s], so_far(c, n, it, 16 * CB, 16 * CB))
                    ch.link(nc.vector.tensor_tensor(fj(v_[s], CB + 1)[:, :, 1:CB + 1], jf(g_[s], CB),
                                                    over_f(w2[:, bass.ds(it * (2 * CB) + s * CB, CB)]), ALU.mult))
                    if not (first(it) and s == 0):
                        dve.wait_ge(q["scanned"], so_far(c, n, it, 2, s))
                    ch.link(nc.vector.tensor_copy(fj(v_[s], CB + 1)[:, :, 0:1], fj(s_[1 - s], CB + 1)[:, :, CB:CB + 1]))
                    dve.wait_ge(q["masked"][s], so_far(c, n, it, 1, 1, 1))
                    if not first(it):
                        dve.wait_ge(q["rowed"], so_far(c, n, it, 2, s - 1))
                    nc.vector.tensor_tensor_scan(s_[s][:, 0:D * (CB + 1)], m_[s][:, 0:D * (CB + 1)],
                                                 v_[s][:, 0:D * (CB + 1)], 0.0, ALU.mult, ALU.add
                                                 ).then_inc(q["scanned"], 1)
                    dve.wait_ge(q["mult"], so_far(c, n, it, 4, s * 2 + 2))
                    if not first(it):
                        for t in range(ST):
                            dve.wait_ge(q["scattered"][t], so_far(c, n, it, 2 * PER, (s - 1) * PER))
                    nc.vector.tensor_tensor(rows(r_[s][:, 0:CB * D]), rows(ps_o[s][:, 0:CB * D]),
                                            over_row(sdd[:, bass.ds(it * (2 * CB) + s * CB, CB)]), ALU.mult
                                            ).then_inc(q["ready"][s], 1)
                ch.end()
            rolled(dve, CN, body, n)
            dve.wait_ge(spread, spread_no[f"f{c}"])
            nc.vector.tensor_copy(tt_[0][0:D, 0:P], ps_c[0:D, 0:P]).then_inc(q["carried"], 1)
            dve.wait_ge(spread, spread_no[f"f{c}"] + 1)
            nc.vector.tensor_scalar(carry[:, :], ps_b[:, 0:D], sdh[:, 0:1], None, ALU.mult).then_inc(q["carried"], 1)

        def fold_pool(pool, c, n, n_less):
            q = fs

            def gather(s, j):
                pool.indirect_dma_start(
                    out=g_[s][:, j * D:(j + 1) * D], out_offset=None, in_=hop_tab[HOPS - 2],
                    in_offset=bass.IndirectOffsetOnAxis(ap=istage[s][:, j:j + 1], axis=0)
                ).then_inc(q["gathered"][s], 16)

            def body(it, more=True):
                for s in range(2):
                    if more:
                        pool.wait_ge(q["staged"][s], so_far(c, n, it, 1, 2, 1))
                    pool.wait_ge(q["ready"][s], so_far(c, n, it, 2, 2))
                    pool.sem_inc(pool_step, 1)
                    for j in range(CB):
                        if more:
                            gather(s, j)
                        scatter(pool, node_sum, eidx_[s][:, j:j + 1], r_[s][:, j * D:(j + 1) * D],
                                q["scattered"], it, s, j, CB, c, n)
            if c > 0:
                pool.indirect_dma_start(out=node_sum[0], out_offset=bass.IndirectOffsetOnAxis(ap=ci32[:, 3:4], axis=0),
                                        in_=zeros[:, 0:D], in_offset=None).then_inc(fixed, 16)
                nfix[0] += 1
                pool.wait_ge(fixed, 16 * nfix[0])
            for s in range(2):
                pool.wait_ge(q["staged"][s], so_far(c, n, 0, 1, 1, 1))
                pool.sem_inc(pool_step, 1)
                for j in range(CB):
                    gather(s, j)
            rolled(pool, CN, body, n_less)
            body(n_less, more=False)
            for t in range(ST):
                pool.wait_ge(q["scattered"][t], n * (2 * PER * (c + 1)))
            pool.wait_ge(q["carried"], 3 * c + 3)
            pool.sem_inc(pool_step, 1)
            pool.indirect_dma_start(out=node_sum[0], out_offset=bass.IndirectOffsetOnAxis(ap=ci32[:, 3:4], axis=0),
                                    in_=carry[:, :], in_offset=None, compute_op=ALU.add).then_inc(fixed, 16)
            nfix[0] += 1
            pool.wait_ge(fixed, 16 * nfix[0])

        PARTS = [4, 4, 4, 2]

        def prod_pe(pe, q, have, c, last_apart=0, centre=False):
            def body(it):
                for s in range(2):
                    rows_in = have(it, s)
                    at = 0
                    for i, m in enumerate(PARTS):
                        no = it * 8 + s * 4 + i
                        if not (first(it) and s == 0 and i < 2):
                            pe.wait_ge(q["cp"], no - 1)
                        for g in range(m):
                            ins = nc.tensor.transpose(ps_t[i % 2][:, g * P:(g + 1) * P],
                                                      rows_in[:, at + g * P:at + (g + 1) * P], ident[:, :])
                        ins.then_inc(q["tr"], 1)
                        at += m * P
                        pe.wait_ge(q["cp"], no + 1)
                        if not (first(it) and s == 0 and i < 2):
                            pe.wait_ge(q["ev"], no - 1)
                        for g in range(m):
                            to = ps_o[i % 2][:, g * P:(g + 1) * P]
                            nc.tensor.matmul(to, xt[i % 2][:, g * P:(g + 1) * P],
                                             bd[:, c * (HOPS + 1) * P:(c * (HOPS + 1) + 1) * P],
                                             start=True, stop=False)
                            ins = nc.tensor.matmul(to, ones[0:1, 0:P], brow[0:1, c * 512:c * 512 + P],
                                                   start=False, stop=True)
                        if centre:
                            for g in range(m):
                                ins = nc.tensor.matmul(ps_x[i % 2][:, g * P:(g + 1) * P],
                                                       xt[i % 2][:, g * P:(g + 1) * P], cmat[:, :],
                                                       start=True, stop=True)
                        ins.then_inc(q["mm"], 1)
            rolled(pe, ITS, body, last_apart=last_apart)

        def prod_act(act, q, it, s):
            for i, m in enumerate(PARTS):
                no = it * 8 + s * 4 + i
                act.wait_ge(q["tr"], no + 1)
                if not (first(it) and s == 0 and i < 2):
                    act.wait_ge(q["mm"], no - 1)
                nc.scalar.copy(xt[i % 2][:, 0:m * P], ps_t[i % 2][:, 0:m * P]).then_inc(q["cp"], 1)

        def x_load(eng, it, s, to, done):
            if isinstance(it, int) and it == ITS - 1 and s == 1:
                b = NBLK - 1
                n0 = b * P * NB
                eng.dma_start(to[0:LASTP, :], x[n0:n0 + LASTP * NB, :].rearrange("(p c) f -> p (c f)", c=NB)
                              ).then_inc(done, 16)
                eng.dma_start(to[LASTP:LASTP + 1, 0:LASTC * D],
                              x[n0 + LASTP * NB:N, :].rearrange("(p c) f -> p (c f)", p=1)).then_inc(done, 16)
            else:
                eng.dma_start(to, node_rows(x, it * 2 + s)).then_inc(done, 16)

        def final(it, s):
            return isinstance(it, int) and it == ITS - 1 and s == 1

        def dense_sp(sp, i):
            q = dense[i]

            def load(it, s):
                tabs = agg_sum if i == 2 else node_sum
                if not first(it):
                    sp.wait_ge(q["var"], (it - 1) * 2 + s + 1)
                sp.dma_start(ub[s], node_rows(tabs[0], it * 2 + s)).then_inc(q["ul"][s], 16)
                sp.dma_start(xb[s], node_rows(tabs[1], it * 2 + s)).then_inc(q["ul"][s], 16)
                if i == 0:
                    if not first(it):
                        sp.wait_ge(q["done"], (it - 1) * 2 + s + 1)
                        sp.sem_inc(sp_step, 1)
                    for k, v in enumerate((gamma, beta)):
                        to = gb[s][:, k * NB:(k + 1) * NB]
                        if final(it, s):
                            n0 = (NBLK - 1) * P * NB
                            sp.dma_start(to[0:LASTP, :], v[n0:n0 + LASTP * NB].rearrange("(p c) -> p c", c=NB)
                                         ).then_inc(gb_in[s], 16)
                            sp.dma_start(to[LASTP:LASTP + 1, 0:LASTC],
                                         v[n0 + LASTP * NB:N].rearrange("(p c) -> p c", p=1)).then_inc(gb_in[s], 16)
                        else:
                            sp.dma_start(to, v[bass.ds((it * 2 + s) * (P * NB), P * NB)].rearrange("(p c) -> p c", p=P)
                                         ).then_inc(gb_in[s], 16)

            def store(it, s):
                b = it * 2 + s
                sp.wait_ge(q["done"], b + 1)
                if i == 0:
                    sp.dma_start(node_rows(node_tab, b), cb[s]).then_inc(q["stored"][s], 16)
                elif i == 1:
                    sp.dma_start(node_rows(node_tab, b), nd[:, bass.ds(b * W, W)]).then_inc(q["stored"][s], 16)
                elif final(it, s):
                    n0 = b * P * NB
                    sp.dma_start(out[n0:n0 + LASTP * NB, :].rearrange("(p c) f -> p (c f)", c=NB),
                                 cb[s][0:LASTP, :]).then_inc(q["stored"][s], 16)
                    sp.dma_start(out[n0 + LASTP * NB:N, :].rearrange("(p c) f -> p (c f)", p=1),
                                 cb[s][LASTP:LASTP + 1, 0:LASTC * D]).then_inc(q["stored"][s], 16)
                else:
                    sp.dma_start(node_rows(out, b), cb[s]).then_inc(q["stored"][s], 16)

            def body(it):
                if not (isinstance(it, int) and it == ITS - 1):
                    for s in range(2):
                        load(it + 1, s)
                for s in range(2):
                    store(it, s)
            for s in range(2):
                load(0, s)
            rolled(sp, ITS, body, last_apart=2)
            sp.wait_ge(q["stored"][0], 16 * ITS)
            sp.wait_ge(q["stored"][1], 16 * (ITS + (i == 2)))

        def dense_act(act, i):
            q = dense[i]

            def body(it):
                for s in range(2):
                    act.wait_ge(q["cen"], it * 2 + s + 1)
                    nc.scalar.activation(ub[s], cb[s], ACT.Square).then_inc(q["sq"], 1)
                for s in range(2):
                    act.wait_ge(q["var"], it * 2 + s + 1)
                    nc.scalar.activation(st[s][:, NB:2 * NB], st[s][:, NB:2 * NB], ACT.Sqrt).then_inc(q["root"], 1)
            rolled(act, ITS, body)

        def dense_pool(pool, i):
            q = dense[i]

            def body(it):
                for s in range(2):
                    pool.wait_ge(q["ul"][s], it * 32 + 32)
                    nc.gpsimd.tensor_tensor(ub[s], ub[s], xb[s], ALU.add).then_inc(q["both"], 1)
                    if i == 1:
                        pool.wait_ge(q["both"], it * 4 + 2 * s + 1)
                        pool.sem_inc(pool_step, 1)
                        nc.gpsimd.tensor_tensor(rows(ub[s]), rows(ub[s]),
                                                over_row(nvs[:, bass.ds((it * 2 + s) * NB, NB)]), ALU.mult
                                                ).then_inc(q["both"], 1)
                if i == 0:
                    for s in range(2):
                        pool.wait_ge(q["scaled"], it * 2 + s + 1)
                        nc.gpsimd.tensor_tensor(rows(cb[s]), rows(cb[s]), over_row(gb[s][:, NB:2 * NB]), ALU.add
                                                ).then_inc(q["shifted"], 1)
            rolled(pool, ITS, body)

        def dense_dve(dve, i):
            q = dense[i]
            ch = Chain(dve, q["chain"])

            def body(it):
                ch.begin(it)
                for s in range(2):
                    b = it * 2 + s
                    blk = nd[:, bass.ds(b * W, W)]
                    if not first(it) and i != 1:
                        dve.wait_ge(q["stored"][s], it * 16)
                    if not first(it) and i == 1:
                        dve.wait_ge(q["done"], it * 2 + s - 1)
                    dve.wait_ge(q["both"], it * 4 + 2 * s + 2 if i == 1 else b + 1)
                    if i == 2:
                        nc.vector.scalar_tensor_tensor(cb[s], blk, 2.0, ub[s], ALU.mult, ALU.add
                                                       ).then_inc(q["cen"], 1)
                    else:
                        nc.vector.tensor_tensor(cb[s], blk, ub[s], ALU.add).then_inc(q["cen"], 1)
                for s in range(2):
                    b = it * 2 + s
                    dve.wait_ge(q["sq"], b + 1)
                    ch.link(nc.vector.tensor_reduce(st[s][:, NB:2 * NB], rows(ub[s]), AX.X, ALU.add))
                    nc.vector.tensor_scalar(st[s][:, NB:2 * NB], st[s][:, NB:2 * NB], 1.0 / D, EPS,
                                            ALU.mult, ALU.add).then_inc(q["var"], 1)
                for s in range(2):
                    b = it * 2 + s
                    dve.wait_ge(q["root"], b + 1)
                    ch.link(nc.vector.reciprocal(st[s][:, NB:2 * NB], st[s][:, NB:2 * NB]))
                    if i == 0:
                        dve.wait_ge(gb_in[s], it * 32 + 32 + (32 if final(it, s) else 0))
                        ch.link(nc.vector.tensor_tensor(st[s][:, NB:2 * NB], st[s][:, NB:2 * NB], gb[s][:, 0:NB],
                                                        ALU.mult))
                    to = nd[:, bass.ds(b * W, W)] if i == 1 else cb[s]
                    nc.vector.tensor_tensor(rows(to), rows(cb[s]), over_row(st[s][:, NB:2 * NB]), ALU.mult
                                            ).then_inc(q["scaled"] if i == 0 else q["done"], 1)
                if i == 0:
                    for s in range(2):
                        dve.wait_ge(q["shifted"], it * 2 + s + 1)
                        nc.vector.scalar_tensor_tensor(cb[s], cb[s], SLOPE, cb[s], ALU.mult, ALU.max
                                                       ).then_inc(q["done"], 1)
                ch.end()
            rolled(dve, ITS, body, last_apart=int(i < 1))

        @block.sync
        def _(sp):
            for a, b, r in ((e_src, src, 16), (e_dst, dst, 16), (e_w, weight, 16)):
                sp.dma_start(b_split(a[0:E], r), b_split(b, r)).then_inc(copied, 16)
            sp.wait_ge(zeroed, 2)
            pad = EP - E
            sp.dma_start(e_src[E:EP].rearrange("(a b) -> a b", a=1), zeros[0:1, 0:pad].bitcast(I32)).then_inc(copied, 16)
            sp.dma_start(e_dst[E:EP + 1].rearrange("(a b) -> a b", a=1), padi[:, :]).then_inc(copied, 16)
            sp.dma_start(e_w[E:EP].rearrange("(a b) -> a b", a=1), zeros[0:1, 0:pad]).then_inc(copied, 16)
            for t in range(LT):
                sp.dma_start(node_lasts[t].rearrange("(p a) b -> p (a b)", p=P), zeros[:, :]).then_inc(tabs0, 16)
            sp.dma_start(edge_info[0:1, :], zeros[0:1, 0:2]).then_inc(tabs0, 16)
            for k in range(HOPS - 1):
                sp.dma_start(hop_tab[k][0:1, :], zeros[0:1, 0:D]).then_inc(tabs0, 16)
                sp.dma_start(hop_tab[k][1 + TROWS:, :], zeros[:, 0:D]).then_inc(tabs0, 16)
            sp.wait_ge(copied, 16 * 6)
            sp.dma_start(e_i[:, 0, :], ev(e_src)).then_inc(loaded, 16)
            sp.dma_start(e_i[:, 1, :], ev(e_dst[0:EP])).then_inc(loaded, 16)
            sp.dma_start(d_next, ev(e_dst[1:EP + 1])).then_inc(loaded, 16)
            sp.dma_start(w_e[:, :], ev(e_w)).then_inc(loaded, 16)
            sp.wait_ge(order_seen, 3)
            unsorted = sp.value_load(ci32[0:1, 3:4], min_val=0, max_val=EP)
            with sp.If(unsorted > 0):
                order_sp(sp)
            sp.wait_ge(tabs0, 16 * (LT + 1 + 2 * (HOPS - 1)))
            phase_end(sp, "sp")
            def load(it, s):
                if not first(it):
                    sp.wait_ge(a0["xst"][s], it * 16)
                x_load(sp, it, s, xb[s], a0["xl"][s])

            def body(it):
                for s in range(2):
                    sp.wait_ge(a0["ev"], it * 8 + s * 4 + 4)
                    sp.sem_inc(sp_step, 1)
                    sp.dma_start(node_rows(x_cent, it * 2 + s), xb[s]).then_inc(a0["xst"][s], 16)
                    for t in node_sum:
                        zero_block(sp, t, it, s)
                    if not (isinstance(it, int) and it == ITS - 1):
                        load(it + 1, s)
            for s in range(2):
                load(0, s)
            rolled(sp, ITS, body, last_apart=2)
            for s in range(2):
                sp.wait_ge(a0["xst"][s], 16 * ITS)
            phase_end(sp, "sp")
            for t in range(LT):
                sp.dma_start(lasts[t], node_lasts[t].rearrange("(p a) b -> p (a b)", p=P)).then_inc(lasts_in, 16)
            sp.wait_ge(lasts_sum, LT)
            sp.dma_start(node_last.rearrange("(p a) b -> p (a b)", p=P), lasts[0]).then_inc(lasts_in, 16)
            sp.wait_ge(lasts_in, 16 * (LT + 1))
            phase_end(sp, "sp")
            def body(it):
                for s in range(2):
                    sp.wait_ge(rg["gathered"][s], it * (16 * EB) + 16 * EB)
                    sp.sem_inc(sp_step, 1)
                    for t in agg_sum:
                        zero_block(sp, t, it, s)
                    for k in range(HOPS - 1):
                        zc = JC * D // NBLK // 4 * 4
                        sp.dma_start(hop_rows(k)[:, bass.ds((it * 2 + s) * zc, zc)].rearrange("p (a b) -> p a b", a=2),
                                     zeros[:, 0:zc // 2].unsqueeze(1).to_broadcast([P, 2, zc // 2])
                                     ).then_inc(big0, 16)
            rolled(sp, ITS, body)
            zc = JC * D // NBLK // 4 * 4
            for k in range(HOPS - 1):
                sp.dma_start(hop_rows(k)[:, NBLK * zc:], zeros[:, 0:JC * D - NBLK * zc]).then_inc(big0, 16)
            for t in node_sum + agg_sum:
                sp.dma_start(t[NP:, :], zeros[:, 0:D]).then_inc(big0, 16)
            phase_end(sp, "sp")
            with sp.If(unsorted < 1):
                attr_copy(sp, e_attr)
            sp.wait_ge(big0, 16 * (NBLK * (2 * ST + HOPS - 1) + HOPS - 1 + 2 * ST))
            phase_end(sp, "sp")
            sp.dma_start(edge_info[1:1 + EP, :].rearrange("(p j) b -> p (j b)", p=P),
                         ei.rearrange("p j b -> p (j b)")).then_inc(info_out, 16)
            sp.wait_ge(info_out, 16)
            phase_end(sp, "sp")
            n = sp.value_load(n_it[0:1, 0:1], min_val=ITS, max_val=CN)
            phase_end(sp, "sp")
            phase_end(sp, "sp")
            for c in range(2):
                for k in range(HOPS - 1):
                    hop_sp(sp, c * (HOPS - 1) + k, n)
                    phase_end(sp, "sp")
                fold_sp(sp, c, n)
                phase_end(sp, "sp")
                dense_sp(sp, c)
                phase_end(sp, "sp")

            def body(it):
                for s in range(2):
                    if not first(it):
                        sp.wait_ge(ls["scanned"], it * 2 + s - 1)
                    sp.dma_start(a_[s], attr_v[:, bass.ds((it * 2 + s) * EB * D, EB * D)]).then_inc(ls["attr"][s], 16)
            rolled(sp, ITS, body)
            phase_end(sp, "sp")
            dense_sp(sp, 2)
            phase_end(sp, "sp")

        @block.gpsimd
        def _(pool):
            pool.memset(ident[:, :], 0.0).then_inc(consts, 1)
            pool.memset(before[:, :], 1.0).then_inc(consts, 1)
            pool.memset(after[:, :], 1.0).then_inc(consts, 1)
            pool.wait_ge(consts, 3)
            pool.affine_select(out=ident[:, :], in_=ident[:, :], compare_op=ALU.not_equal, fill=1.0, base=0,
                               pattern=[[-1, P]], channel_multiplier=1)
            pool.affine_select(out=before[:, :], in_=before[:, :], compare_op=ALU.is_gt, fill=0.0, base=0,
                               pattern=[[1, P]], channel_multiplier=-1)
            pool.affine_select(out=after[:, :], in_=after[:, :], compare_op=ALU.is_gt, fill=0.0, base=0,
                               pattern=[[-1, P]], channel_multiplier=1)
            pool.iota(col_i[:, :], [[1, JC]], base=1, channel_multiplier=0, allow_small_or_imprecise_dtypes=True)
            pool.iota(edge_no[:, :], [[1, J]], base=1, channel_multiplier=J, allow_small_or_imprecise_dtypes=True)
            for i, (b, m) in enumerate(((N, 1), (1 + TROWS, 1), (0, JC), (0, J))):
                pool.iota(part_c[:, i:i + 1], [[0, 1]], base=b, channel_multiplier=m,
                          allow_small_or_imprecise_dtypes=True)
            pool.drain().then_inc(consts_ready, 1)
            pool.wait_ge(order_seen, 3)
            unsorted = pool.value_load(ci32[0:1, 3:4], min_val=0, max_val=EP)
            with pool.If(unsorted > 0):
                order_pool(pool)
            phase_end(pool, "pool")

            def body(it):
                for s in range(2):
                    pool.wait_ge(rs["staged"][s], it * 2 + 2)
                    pool.sem_inc(pool_step, 1)
                    for j in range(EB):
                        scatter(pool, node_lasts, istage[s][:, j:j + 1], st[s][:, j:j + 1],
                                rs["scattered"], it, s, j, EB)
            rolled(pool, ITS, body)
            for t in range(LT):
                pool.wait_ge(rs["scattered"][t], ITS * 2 * EB // LT * 16)
            phase_end(pool, "pool")
            phase_end(pool, "pool")

            def body(it):
                for s in range(2):
                    pool.wait_ge(rg["staged"][s], it + 1)
                    pool.sem_inc(pool_step, 1)
                    for j in range(EB):
                        pool.indirect_dma_start(
                            out=st[s][:, j:j + 1], out_offset=None, in_=node_last,
                            in_offset=bass.IndirectOffsetOnAxis(ap=istage[s][:, j:j + 1], axis=0)
                        ).then_inc(rg["gathered"][s], 16)
            rolled(pool, ITS, body)
            phase_end(pool, "pool")
            phase_end(pool, "pool")
            phase_end(pool, "pool")
            n = pool.value_load(n_it[0:1, 0:1], min_val=ITS, max_val=CN)
            n_less = pool.value_load(n_it[0:1, 1:2], min_val=ITS - 1, max_val=CN - 1)

            def body(it):
                for s in range(2):
                    pool.wait_ge(eg_s["staged"][s], it + 1)
                    pool.sem_inc(pool_step, 1)
                    for j in range(CB):
                        pool.indirect_dma_start(
                            out=st[s][:, 2 * j:2 * j + 2], out_offset=None, in_=edge_info,
                            in_offset=bass.IndirectOffsetOnAxis(ap=istage[s][:, j:j + 1], axis=0)
                        ).then_inc(eg_s["gathered"][s], 16)
            rolled(pool, CN, body, n)
            phase_end(pool, "pool")
            phase_end(pool, "pool")
            for c in range(2):
                for k in range(HOPS - 1):
                    hop_pool(pool, c * (HOPS - 1) + k, n)
                    phase_end(pool, "pool")
                fold_pool(pool, c, n, n_less)
                phase_end(pool, "pool")
                dense_pool(pool, c)
                phase_end(pool, "pool")

            def l_gather(s, j):
                pool.indirect_dma_start(
                    out=g_[s][:, j * D:(j + 1) * D], out_offset=None, in_=node_tab,
                    in_offset=bass.IndirectOffsetOnAxis(ap=istage[s][:, j:j + 1], axis=0)
                ).then_inc(ls["gathered"][s], 16)

            pool.wait_ge(ls["staged"][0], 1)
            for j in range(EB):
                l_gather(0, j)

            def body(it):
                for s in range(2):
                    more = not (isinstance(it, int) and it == ITS - 1 and s == 1)
                    if more:
                        pool.wait_ge(ls["staged"][1 - s], it + s + 1)
                        pool.sem_inc(pool_step, 1)
                    for j in range(EB + LEAD):
                        if more and j < EB:
                            l_gather(1 - s, j)
                        if j == LEAD:
                            pool.wait_ge(ls["ready"][s], it * 2 + 2)
                            pool.sem_inc(pool_step, 1)
                        if j >= LEAD:
                            scatter(pool, agg_sum, eidx_[s][:, j - LEAD:j - LEAD + 1],
                                    r_[s][:, (j - LEAD) * D:(j - LEAD + 1) * D], ls["scattered"], it, s, j - LEAD, EB)
            rolled(pool, ITS, body, last_apart=1)
            for t in range(ST):
                pool.wait_ge(ls["scattered"][t], ITS * 2 * EB // ST * 16)
            pool.wait_ge(ls["carried"], 1)
            pool.indirect_dma_start(out=agg_sum[0], out_offset=bass.IndirectOffsetOnAxis(ap=ci32[:, 0:1], axis=0),
                                    in_=carry[:, :], in_offset=None, compute_op=ALU.add).then_inc(fixed, 16)
            nfix[0] += 1
            pool.wait_ge(fixed, 16 * nfix[0])
            phase_end(pool, "pool")
            dense_pool(pool, 2)
            phase_end(pool, "pool")

        @block.scalar
        def _(act):
            act.wait_ge(bd0, 2)
            for l, (w, b) in enumerate(((W0, b0), (W1, b1))):
                for k in range(HOPS + 1):
                    for g in range(GC):
                        c0 = (l * (HOPS + 1) + k) * P + g * D
                        act.dma_start(bd[g * D:(g + 1) * D, c0:c0 + D], w[k, :, :]).then_inc(wts, 16)
                for g in range(512 // D):
                    act.dma_start(brow[0:1, l * 512 + g * D:l * 512 + (g + 1) * D],
                                  b.rearrange("(a f) -> a f", a=1)).then_inc(wts, 16)
            nb1 = (NBLK - 1) * NB
            act.dma_start(nvs[:, 0:nb1].rearrange("p (b c) -> p b c", c=NB),
                          nv[0:nb1 * P].rearrange("(b p c) -> p b c", p=P, c=NB)).then_inc(wts, 16)
            n0 = nb1 * P
            act.dma_start(nvs[0:LASTP, nb1:], nv[n0:n0 + LASTP * NB].rearrange("(p c) -> p c", c=NB)).then_inc(wts, 16)
            act.dma_start(nvs[LASTP:LASTP + 1, nb1:nb1 + LASTC],
                          nv[n0 + LASTP * NB:N].rearrange("(p c) -> p c", p=1)).then_inc(wts, 16)
            act.wait_ge(wts, 16 * (2 * (HOPS + 1) * GC + 2 * 512 // D + 3))
            act.sem_inc(wts_done, 1)
            phase_end(act, "act")

            def body(it):
                for s in range(2):
                    if not first(it):
                        for t in range(LT):
                            act.wait_ge(rs["scattered"][t], (it * 2 + s - 1) * (EB // LT * 16))
                    nc.scalar.copy(istage[s][:, :], sidx[:, bass.ds((it * 2 + s) * EB, EB)]).then_inc(rs["staged"][s], 1)
                    nc.scalar.copy(st[s][:, 0:EB], edge_no[:, bass.ds((it * 2 + s) * EB, EB)]
                                   ).then_inc(rs["staged"][s], 1)
                    prod_act(act, a0, it, s)
            rolled(act, ITS, body)
            phase_end(act, "act")
            phase_end(act, "act")

            def stage(it, s):
                nc.scalar.copy(istage[s][:, :], e_i[:, 0, bass.ds((it * 2 + s) * EB, EB)]).then_inc(rg["staged"][s], 1)

            def body(it):
                for s in range(2):
                    act.wait_ge(rg["gathered"][s], it * (16 * EB) + 16 * EB)
                    nc.scalar.copy(rv[:, bass.ds((it * 2 + s) * EB, EB)], st[s][:, 0:EB]).then_inc(act_own, 1)
                    act.wait_ge(act_own, it * 2 + s + 1)
                    if not (isinstance(it, int) and it == ITS - 1):
                        stage(it + 1, s)
            for s in range(2):
                stage(0, s)
            rolled(act, ITS, body, last_apart=1)
            phase_end(act, "act")
            act.wait_ge(root_in, 1)
            nc.scalar.activation(sdd[:, :], sdd[:, :], ACT.Sqrt).then_inc(root_out, 1)
            phase_end(act, "act")
            phase_end(act, "act")
            n = act.value_load(n_it[0:1, 0:1], min_val=ITS, max_val=CN)

            def stage2(it, s):
                nc.scalar.copy(istage[s][:, 0:CB], gidx[:, bass.ds((it * 2 + s) * CB, CB)]).then_inc(eg_s["staged"][s], 1)

            def body(it):
                for s in range(2):
                    act.wait_ge(eg_s["gathered"][s], it * (16 * CB) + 16 * CB)
                    nc.scalar.copy(eg[:, bass.ds((it * 2 + s) * CB, CB), :],
                                   st[s][:, 0:2 * CB].rearrange("p (j b) -> p j b", b=2)).then_inc(act_own, 1)
                    act.wait_ge(act_own, it * 2 + s + 1 + NBLK)
                    stage2(it + 1, s)
            for s in range(2):
                stage2(0, s)
            rolled(act, CN, body, n)
            phase_end(act, "act")
            act.wait_ge(root_in, 2)
            nc.scalar.activation(live[:, :], live[:, :], ACT.Sqrt).then_inc(root_out, 1)
            phase_end(act, "act")
            for c in range(2):
                for k in range(HOPS - 1):
                    hop_act(act, c * (HOPS - 1) + k, n)
                    phase_end(act, "act")
                fold_act(act, c, n)
                phase_end(act, "act")
                dense_act(act, c)
                phase_end(act, "act")

            def stage3(it, s):
                nc.scalar.copy(istage[s][:, :], e_i[:, 0, bass.ds((it * 2 + s) * EB, EB)]).then_inc(ls["staged"][s], 1)
                nc.scalar.copy(fj(m_[s], EB + 1),
                               over_f(maske[:, bass.ds((it * 2 + s) * (EB + 1), EB + 1)])).then_inc(ls["masked"][s], 1)

            def body(it):
                for s in range(2):
                    act.wait_ge(ls["scanned"], it * 2 + s + 1)
                    if not first(it):
                        for t in range(ST):
                            act.wait_ge(ls["scattered"][t], (it * 2 + s - 1) * (16 * EB // ST))
                    nc.scalar.copy(eidx_[s][:, :], sidx[:, bass.ds((it * 2 + s) * EB, EB)]).then_inc(ls["ready"][s], 1)
                    if not (isinstance(it, int) and it == ITS - 1):
                        stage3(it + 1, s)
            for s in range(2):
                stage3(0, s)
            rolled(act, ITS, body, last_apart=1)
            phase_end(act, "act")
            dense_act(act, 2)
            phase_end(act, "act")

        @block.tensor
        def _(pe):
            pe.wait_ge(order_seen, 1)
            nc.tensor.matmul(ps_c[0:1, 0:1], sm[:, 9:10], ones[:, 0:1], start=True, stop=True
                             ).then_inc(order_seen, 1)
            pe.wait_ge(consts_ready, 1)
            pe.wait_ge(cols_ready, 1)
            for i in range(2):
                ins = nc.tensor.matmul(ps_b[:, i * P:(i + 1) * P], lb[:, i * P:(i + 1) * P], ident[:, :],
                                       start=True, stop=True)
            ins.then_inc(spread, 1)
            pe.wait_ge(cols_ready, 2)
            nc.tensor.matmul(ps_c[:, 0:2], mat[:, :], sm[:, 2:4], start=True, stop=True).then_inc(spread, 1)
            pe.wait_ge(cols_ready, 3)
            nc.tensor.matmul(ps_c[:, 2:3], mat2[:, :], sm[:, 10:11], start=True, stop=True).then_inc(spread, 1)
            phase_end(pe, "pe")

            def have(it, s):
                if isinstance(it, int) and it == ITS - 1 and s == 1:
                    pe.wait_ge(a0["xl"][s], ITS * 16 + 16)
                else:
                    pe.wait_ge(a0["xl"][s], it * 16 + 16)
                return xb[s]
            pe.wait_ge(centred, 1)
            prod_pe(pe, a0, have, 0, last_apart=1, centre=True)
            phase_end(pe, "pe")
            phase_end(pe, "pe")
            phase_end(pe, "pe")
            pe.wait_ge(cols_ready, 4)
            for i in range(4):
                ins = nc.tensor.matmul(ps_b[:, i * P:(i + 1) * P], lb[:, i * P:(i + 1) * P], ident[:, :],
                                       start=True, stop=True)
            ins.then_inc(spread, 1)
            phase_end(pe, "pe")
            phase_end(pe, "pe")
            n = pe.value_load(n_it[0:1, 0:1], min_val=ITS, max_val=CN)
            phase_end(pe, "pe")
            phase_end(pe, "pe")
            for c in range(2):
                for k in range(HOPS - 1):
                    hop_pe(pe, c * (HOPS - 1) + k, n)
                    phase_end(pe, "pe")
                fold_pe(pe, c, n)
                phase_end(pe, "pe")
                phase_end(pe, "pe")
            pe.wait_ge(ls["scanned"], NBLK)
            nc.tensor.matmul(ps_c[:, 0:D], mat[:, :], fj(s_[1], EB + 1)[:, :, EB], start=True, stop=True
                             ).then_inc(spread, 1)
            phase_end(pe, "pe")
            phase_end(pe, "pe")

        @block.vector
        def _(dve):
            ch = Chain(dve, "dve_chain")
            V = nc.vector

            def tt(o, a, b, op):
                ch.link(V.tensor_tensor(o, a, b, op))

            def ts(o, a, s1, s2, o1, o2=None):
                ch.link(V.tensor_scalar(o, a, s1, s2, o1, o2) if o2 is not None else V.tensor_scalar(o, a, s1, s2, o1))

            def cp(o, a):
                ch.link(V.tensor_copy(o, a))

            def red(o, a, op=ALU.add):
                ch.link(V.tensor_reduce(o, a, AX.X, op))

            def rsqrt0(o, a, tmp, no):
                ts(tmp, a, 0.0, None, ALU.is_gt)
                V.tensor_scalar(o, a, 1.2e-38, None, ALU.max).then_inc(root_in, 1)
                dve.wait_ge(root_out, no)
                ch.link(V.reciprocal(o, o))
                tt(o, o, tmp, ALU.mult)

            head_c = pay[:, 0, :]

            def c_(i):
                return sm[:, i:i + 1]
            FIRST, LAST, PD, PC, CD, CC, CONT, HV, CF, T0, DEGEND, RCH, INITR = range(13)
            POS, FC, LC, CNT, CARP, CONTC, HVC, CFC = range(16, 24)

            V.memset(zeros[:, :], 0.0).then_inc(zeroed, 1)
            V.memset(padi[:, :], int(PADV)).then_inc(zeroed, 1)
            V.memset(ones[:, :], 1.0)
            V.memset(bd[:, :], 0.0).then_inc(bd0, 1)
            V.memset(nvs[:, :], 0.0).then_inc(bd0, 1)
            for t in (gidx, srcc, ridx, uidx):
                V.memset(t[:, JC:JX], 0)
            V.memset(w1[:, JC:JX], 0.0)
            V.memset(w2[:, JC:JX], 0.0)
            V.memset(eg[:, :, :], 0.0)
            V.memset(maskc[:, :], 0.0)
            V.memset(maske[:, :], 0.0)
            ch.link(V.memset(same[:, 0:1], 1.0))
            dve.wait_ge(loaded, 64)
            cp(d_e[:, :], e_i[:, 1, :])
            cp(t_f[:, 0:J], d_next)
            tt(t_e[:, 0:J], d_e[:, :], t_f[:, 0:J], ALU.is_gt)
            red(c_(T0), t_e[:, 0:J])
            dve.sem_inc(order_seen, 1)
            dve.wait_ge(order_seen, 2)
            cp(ci32[0:1, 3:4], ps_c[0:1, 0:1])
            dve.sem_inc(order_seen, 1)
            unsorted = dve.value_load(ci32[0:1, 3:4], min_val=0, max_val=EP)
            dve.wait_ge(consts_ready, 1)
            with dve.If(unsorted > 0):
                order_dve(dve)
            tt(same[:, 1:J], d_e[:, 1:J], d_e[:, 0:J - 1], ALU.is_equal)
            cp(c_(FIRST), d_e[:, 0:1])
            cp(c_(LAST), d_e[:, J - 1:J])
            cp(lb[:, 0:P], c_(FIRST).to_broadcast([P, P]))
            V.tensor_copy(lb[:, P:2 * P], c_(LAST).to_broadcast([P, P])).then_inc(cols_ready, 1)
            cp(maske[:, 0:(J // EB) * (EB + 1)].rearrange("p (b j) -> p b j", j=EB + 1)[:, :, 1:EB + 1],
               same[:, :].rearrange("p (b j) -> p b j", j=EB))
            ch.link(V.tensor_tensor_scan(deg[:, :], same[:, :], w_e[:, :], 0.0, ALU.mult, ALU.add))
            ch.link(V.tensor_tensor_scan(cnt[:, :], same[:, :], ones[:, :], 0.0, ALU.mult, ALU.add))
            cp(c_(PD), deg[:, J - 1:J])
            cp(c_(PC), cnt[:, J - 1:J])
            dve.wait_ge(spread, spread_no["r1"])
            ch.link(V.scalar_tensor_tensor(mat[:, :], ps_b[:, 0:P], c_(LAST), before[:, :], ALU.is_equal, ALU.mult))
            V.scalar_tensor_tensor(mat2[:, :], ps_b[:, P:2 * P], c_(FIRST), after[:, :], ALU.is_equal, ALU.mult
                                   ).then_inc(cols_ready, 1)
            dve.wait_ge(cols_ready, 2)
            red(c_(CONT), mat[:, :])
            ts(c_(CONT), c_(CONT), 0.5, None, ALU.is_gt)
            ch.link(V.memset(last[:, J - 1:J], 1.0))
            tt(last[:, 0:J - 1], d_e[:, 0:J - 1], d_e[:, 1:J], ALU.not_equal)
            ts(t_e[:, 0:J], d_e[:, :], c_(LAST), c_(CONT), ALU.is_equal, ALU.mult)
            ts(t_e[:, 0:J], t_e[:, 0:J], -1.0, 1.0, ALU.mult, ALU.add)
            tt(last[:, :], last[:, :], t_e[:, 0:J], ALU.mult)
            ts(t_e[:, 0:J], d_e[:, :], float(N), None, ALU.is_lt)
            tt(last[:, :], last[:, :], t_e[:, 0:J], ALU.mult)
            ts(head[:, :], d_e[:, :], c_(FIRST), None, ALU.is_equal)
            dve.wait_ge(spread, spread_no["r2"])
            cp(sm[:, CD:CD + 2], ps_c[:, 0:2])
            ch.link(V.tensor_tensor_scan(deg[:, :], same[:, :], w_e[:, :], c_(CD), ALU.mult, ALU.add))
            ch.link(V.tensor_tensor_scan(cnt[:, :], same[:, :], ones[:, :], c_(CC), ALU.mult, ALU.add))
            ts(rcnt[:, :], cnt[:, :], 1.0, None, ALU.max)
            ch.link(V.reciprocal(rcnt[:, :], rcnt[:, :]))
            tt(rcnt[:, :], rcnt[:, :], last[:, :], ALU.mult)
            tt(head[:, :], head[:, :], last[:, :], ALU.mult)
            red(c_(HV), head[:, :])
            tt(t_e[:, 0:J], head[:, :], deg[:, :], ALU.mult)
            red(c_(DEGEND), t_e[:, 0:J])
            tt(t_e[:, 0:J], head[:, :], rcnt[:, :], ALU.mult)
            red(c_(RCH), t_e[:, 0:J])
            dve.sem_inc(cols_ready, 1)
            tt(c_(T0), c_(FIRST), part_c[:, 0:1], ALU.subtract)
            tt(c_(T0), c_(T0), c_(HV), ALU.mult)
            tt(c_(T0), c_(T0), part_c[:, 0:1], ALU.add)
            cp(ci32[:, 0:1], c_(T0))
            ts(t_e[:, 0:J], d_e[:, :], part_c[:, 0:1], None, ALU.subtract)
            tt(t_e[:, 0:J], t_e[:, 0:J], last[:, :], ALU.mult)
            ts(t_e[:, 0:J], t_e[:, 0:J], part_c[:, 0:1], None, ALU.add)
            cp(sidx[:, :], t_e[:, 0:J])
            dve.wait_ge(spread, spread_no["r3"])
            cp(c_(INITR), ps_c[:, 2:3])
            tt(t_e[:, 0:J], last[:, :], deg[:, :], ALU.mult)
            ts(t_f[:, 0:J], last[:, :], -1.0, 1.0, ALU.mult, ALU.add)
            ch.link(V.tensor_tensor_scan(ddst[:, ::-1], t_f[:, 0:J][:, ::-1], t_e[:, 0:J][:, ::-1], c_(INITR),
                                         ALU.mult, ALU.add))
            dve.wait_ge(wts_done, 1)
            n_g = 2 * (HOPS + 1) * GC
            for t, g, pp in ((bd, n_g, P), (cmat, GC, P), (brow, 2 * 512 // D, 1)):
                if t is cmat:
                    cp(cmat[:, :], ident[:, :])
                v = t[0:pp, :].rearrange("p (g f) -> p g f", f=D)
                red(t_e[0:pp, 0:g], v)
                ts(t_e[0:pp, 0:g], t_e[0:pp, 0:g], 1.0 / D, None, ALU.mult)
                tt(v, v, t_e[0:pp, 0:g].unsqueeze(2).to_broadcast([pp, g, D]), ALU.subtract)
            dve.sem_inc(centred, 1)
            phase_end(dve, "dve")

            def body(it):
                for s in range(2):
                    o = 0
                    for i, m in enumerate(PARTS):
                        dve.wait_ge(a0["mm"], it * 8 + s * 4 + i + 1)
                        V.tensor_copy(nd[:, bass.ds((it * 2 + s) * W + o, m * P)], ps_o[i % 2][:, 0:m * P])
                        V.tensor_copy(xb[s][:, o:o + m * P], ps_x[i % 2][:, 0:m * P]).then_inc(a0["ev"], 1)
                        o += m * P
            rolled(dve, ITS, body)
            phase_end(dve, "dve")
            dve.wait_ge(lasts_in, 16 * LT)
            for t in range(1, LT):
                V.tensor_tensor(lasts[0], lasts[0], lasts[t], ALU.add).then_inc(lasts_sum, 1)
                dve.wait_ge(lasts_sum, t)
            dve.sem_inc(lasts_sum, 1)
            phase_end(dve, "dve")
            phase_end(dve, "dve")

            ch.link(V.memset(pay[:, :, :], 0.0))
            ch.link(V.memset(live[:, :], 0.0))
            ch.link(V.memset(sh[:, :, :], 0))
            ts(live[:, 0:J], rv[:, :], 0.5, None, ALU.is_gt)
            ts(t_e[:, 0:J], d_e[:, :], float(N), None, ALU.is_lt)
            tt(live[:, 0:J], live[:, 0:J], t_e[:, 0:J], ALU.mult)
            ch.link(V.tensor_tensor_scan(t_e[:, 0:J], ones[:, :], live[:, 0:J], 0.0, ALU.mult, ALU.add))
            cp(c_(CNT), t_e[:, J - 1:J])
            ts(t_f[:, 0:J], t_e[:, 0:J], part_c[:, 2:3], None, ALU.add)
            tt(t_f[:, 0:J], t_f[:, 0:J], live[:, 0:J], ALU.mult)
            cp(head[:, :], t_f[:, 0:J])
            tt(t_f[:, 0:J], col_i[:, 0:J], t_e[:, 0:J], ALU.subtract)
            tt(t_f[:, 0:J], t_f[:, 0:J], live[:, 0:J], ALU.mult)
            cp(sh[:, 0, 0:J], t_f[:, 0:J])
            cp(pay[:, 0, 0:J], rv[:, :])
            cp(pay[:, 1, 0:J], w_e[:, :])
            cp(pay[:, 2, 0:J], d_e[:, :])
            cp(pay[:, 3, 0:J], ddst[:, :])
            cp(pay[:, 4, 0:J], e_i[:, 0, :])
            cur = 0
            for b in range(9):
                k = 1 << b
                ts(mv[:, :], sh[:, cur, :], k, None, ALU.bitwise_and)
                ch.link(V.copy_predicated(pay[:, :, 0:JC - k], mv[:, k:JC].unsqueeze(1).to_broadcast([P, 5, JC - k]),
                                          pay[:, :, k:JC]))
                ch.link(V.scalar_tensor_tensor(sh[:, 1 - cur, :], mv[:, :], 0.0, sh[:, cur, :],
                                               ALU.is_equal, ALU.mult))
                ch.link(V.copy_predicated(sh[:, 1 - cur, 0:JC - k], mv[:, k:JC], sh[:, cur, k:JC]))
                cur = 1 - cur
            ts(live[:, :], col_i[:, :], c_(CNT), None, ALU.is_le)
            for i in (0, 1, 3, 4):
                tt(pay[:, i, :], pay[:, i, :], live[:, :], ALU.mult)
            ts(t_e[:, :], pay[:, 2, :], 1.0, None, ALU.add)
            tt(t_e[:, :], t_e[:, :], live[:, :], ALU.mult)
            red(c_(LC), t_e[:, :], ALU.max)
            ts(c_(LC), c_(LC), -1.0, None, ALU.add)
            ts(t_e[:, :], pay[:, 2, :], PADV, None, ALU.subtract)
            tt(t_e[:, :], t_e[:, :], live[:, :], ALU.mult)
            ts(pay[:, 2, :], t_e[:, :], PADV, None, ALU.add)
            cp(gidx[:, 0:JC], pay[:, 0, :])
            dc = pay[:, 2, :]
            cp(c_(FC), pay[:, 2, 0:1])
            tt(c_(POS), c_(CNT), part_c[:, 2:3], ALU.add)
            for i, m in enumerate((FC, LC, POS, CNT)):
                cp(lb[:, i * P:(i + 1) * P], c_(m).to_broadcast([P, P]))
            dve.sem_inc(cols_ready, 1)
            dve.wait_ge(spread, spread_no["r4"])
            ch.link(V.scalar_tensor_tensor(matc[:, :], ps_b[:, 0:P], c_(LC), before[:, :], ALU.is_equal, ALU.mult))
            red(c_(CONTC), matc[:, :])
            ts(c_(CONTC), c_(CONTC), 0.5, None, ALU.is_gt)
            ch.link(V.scalar_tensor_tensor(lb[:, 0:P], ps_b[:, P:2 * P], c_(FIRST), after[:, :],
                                           ALU.is_equal, ALU.mult))
            tt(lb[:, 0:P], lb[:, 0:P], ps_b[:, 2 * P:3 * P], ALU.mult)
            red(c_(CARP), lb[:, 0:P], ALU.max)
            ch.link(V.tensor_tensor_scan(t_e[:, 0:J], same[:, :], head[:, :], c_(CARP), ALU.mult, ALU.max))
            cp(ei[:, :, 0], t_e[:, 0:J])
            cp(ei[:, :, 1], deg[:, :])
            red(c_(T0), ps_b[:, 3 * P:4 * P], ALU.max)
            ts(c_(T0), c_(T0), float(2 * CB * (ITS - 1) + 1), float(2 * CB - 1), ALU.max, ALU.add)
            cp(ci32[:, 2:3], c_(T0))
            ch.link(V.tensor_scalar(n_it[0:1, 0:1], ci32[0:1, 2:3], (2 * CB).bit_length() - 1, None,
                                    ALU.logical_shift_right))
            cp(sm[0:1, T0:T0 + 1], n_it[0:1, 0:1])
            ts(sm[0:1, T0:T0 + 1], sm[0:1, T0:T0 + 1], -1.0, None, ALU.add)
            cp(n_it[0:1, 1:2], sm[0:1, T0:T0 + 1])
            ch.link(V.memset(samec[:, 0:1], 1.0))
            tt(samec[:, 1:JC], pay[:, 2, 1:JC], pay[:, 2, 0:JC - 1], ALU.is_equal)
            ts(t_e[:, :], live[:, :], -1.0, 1.0, ALU.mult, ALU.add)
            tt(samec[:, :], samec[:, :], t_e[:, :], ALU.max)
            cp(maskc[:, 0:(JC // CB) * (CB + 1)].rearrange("p (b j) -> p b j", j=CB + 1)[:, :, 1:CB + 1],
               samec[:, :].rearrange("p (b j) -> p b j", j=CB))
            ch.link(V.memset(lastc[:, JC - 1:JC], 1.0))
            tt(lastc[:, 0:JC - 1], pay[:, 2, 0:JC - 1], pay[:, 2, 1:JC], ALU.not_equal)
            ts(t_e[:, :], dc, c_(LC), c_(CONTC), ALU.is_equal, ALU.mult)
            ts(t_e[:, :], t_e[:, :], -1.0, 1.0, ALU.mult, ALU.add)
            tt(lastc[:, :], lastc[:, :], t_e[:, :], ALU.mult)
            tt(lastc[:, :], lastc[:, :], live[:, :], ALU.mult)
            ts(t_e[:, :], dc, c_(FC), None, ALU.is_equal)
            tt(t_e[:, :], t_e[:, :], live[:, :], ALU.mult)
            red(c_(CFC), t_e[:, :])
            tt(head_c, t_e[:, :], lastc[:, :], ALU.mult)
            red(c_(HVC), head_c)
            tt(c_(T0), c_(FC), part_c[:, 0:1], ALU.subtract)
            tt(c_(T0), c_(T0), c_(HVC), ALU.mult)
            tt(c_(T0), c_(T0), part_c[:, 0:1], ALU.add)
            cp(ci32[:, 3:4], c_(T0))
            tt(c_(T0), c_(CFC), part_c[:, 2:3], ALU.add)
            tt(c_(T0), c_(T0), part_c[:, 1:2], ALU.subtract)
            tt(c_(T0), c_(T0), c_(HVC), ALU.mult)
            tt(c_(T0), c_(T0), part_c[:, 1:2], ALU.add)
            cp(ci32[:, 1:2], c_(T0))
            ts(t_e[:, :], dc, part_c[:, 0:1], None, ALU.subtract)
            tt(t_e[:, :], t_e[:, :], lastc[:, :], ALU.mult)
            ts(t_e[:, :], t_e[:, :], part_c[:, 0:1], None, ALU.add)
            cp(uidx[:, 0:JC], t_e[:, :])
            cp(srcc[:, 0:JC], pay[:, 4, :])
            rsqrt0(sdd[:, :], pay[:, 3, :], t_e[:, :], 1)
            tt(t_e[:, :], head_c, sdd[:, :], ALU.mult)
            red(sdh[:, 0:1], t_e[:, :])
            phase_end(dve, "dve")
            phase_end(dve, "dve")
            n = dve.value_load(n_it[0:1, 0:1], min_val=ITS, max_val=CN)
            phase_end(dve, "dve")
            cp(ridx[:, 0:JC], eg[:, 0:JC, 0])
            cp(t_f[:, :], eg[:, 0:JC, 1])
            rsqrt0(live[:, :], t_f[:, :], t_e[:, :], 2)
            tt(w1[:, 0:JC], pay[:, 1, :], live[:, :], ALU.mult)
            tt(w2[:, 0:JC], w1[:, 0:JC], live[:, :], ALU.mult)
            phase_end(dve, "dve")
            hop_chain.append(Chain(dve, "hop_chain"))
            fold_chain.append(Chain(dve, "fold_chain"))
            for c in range(2):
                for k in range(HOPS - 1):
                    hop_dve(dve, c * (HOPS - 1) + k, n)
                    phase_end(dve, "dve")
                fold_dve(dve, c, n)
                phase_end(dve, "dve")
                dense_dve(dve, c)
                phase_end(dve, "dve")

            lc = Chain(dve, "l_chain")
            V.memset(s_[1][:, :], 0.0).then_inc(l0, 1)
            dve.wait_ge(l0, 1)

            def body(it):
                lc.begin(it)
                for s in range(2):
                    dve.wait_ge(ls["gathered"][s], it * (16 * EB) + 16 * EB)
                    dve.wait_ge(ls["attr"][s], it * 16 + 16)
                    lc.link(V.tensor_tensor(fj(v_[s], EB + 1)[:, :, 1:EB + 1], jf(g_[s], EB), jf(a_[s], EB), ALU.mult))
                    if not (first(it) and s == 0):
                        dve.wait_ge(ls["scanned"], it * 2 + s)
                    lc.link(V.tensor_copy(fj(v_[s], EB + 1)[:, :, 0:1], fj(s_[1 - s], EB + 1)[:, :, EB:EB + 1]))
                    dve.wait_ge(ls["masked"][s], it + 1)
                    V.tensor_tensor_scan(s_[s], m_[s], v_[s], 0.0, ALU.mult, ALU.add).then_inc(ls["scanned"], 1)
                    dve.wait_ge(ls["scanned"], it * 2 + s + 1)
                    if not first(it):
                        for t in range(ST):
                            dve.wait_ge(ls["scattered"][t], (it * 2 + s - 1) * (16 * EB // ST))
                    sums = fj(s_[s], EB + 1)[:, :, 1:EB + 1]
                    lc.link(V.tensor_tensor(jf(r_[s], EB), sums, over_f(rcnt[:, bass.ds((it * 2 + s) * EB, EB)]),
                                            ALU.mult))
                    lc.link(V.tensor_reduce(st[s][:, 0:EB], rows(r_[s]), AX.X, ALU.add))
                    lc.link(V.tensor_scalar(st[s][:, 0:EB], st[s][:, 0:EB], 1.0 / D, None, ALU.mult))
                    V.tensor_tensor(rows(r_[s]), rows(r_[s]), over_row(st[s][:, 0:EB]), ALU.subtract
                                    ).then_inc(ls["ready"][s], 1)
                lc.end()
            rolled(dve, ITS, body)
            dve.wait_ge(spread, spread_no["l1"])
            ts(carry[:, :], ps_c[:, 0:D], c_(RCH), None, ALU.mult)
            red(c_(T0), carry[:, :])
            ts(c_(T0), c_(T0), 1.0 / D, None, ALU.mult)
            ts(carry[:, :], carry[:, :], c_(T0), None, ALU.subtract)
            dve.sem_inc(ls["carried"], 1)
            phase_end(dve, "dve")
            dense_dve(dve, 2)
            phase_end(dve, "dve")


_INS = ["x", "src", "dst", "edge_attr_32", "edge_weight", "node_vec",
        "node_vec_n2", "node_vec_n3",
        "L0_gnn_W0", "L0_gnn_b0", "L0_gnn_W1", "L0_gnn_b1"]


def kernel(**inputs):
    import numpy as np
    import concourse.bacc as bacc
    from concourse.bass_utils import run_bass_kernel_spmd

    nc = bacc.Bacc("TRN2", target_bir_lowering=False, num_devices=1)
    arrays, args = {}, []
    for name in _INS:
        a = np.ascontiguousarray(inputs[name])
        arrays[f"in_{name}"] = a
        args.append(nc.dram_tensor(f"in_{name}", a.shape, mybir.dt.from_np(a.dtype), kind="ExternalInput").ap())
    args.append(nc.dram_tensor("out_rows", (N, D), F32, kind="ExternalOutput").ap())
    gnn_program(nc, *args)
    r = run_bass_kernel_spmd(nc, [arrays], core_ids=[0])
    return r.results[0]["out_rows"]
```
